# Optimizing a Trainium2 kernel written in Bass

```python
import numpy as np
import jax
import jax.numpy as jnp

def _softmax(x, axis=-1):
    return jax.nn.softmax(x, axis=axis)

def _gelu(x):
    return jax.nn.gelu(x, approximate=True)

def _silu(x):
    return jax.nn.silu(x)

def _sigmoid(x):
    return jax.nn.sigmoid(x)

def _layernorm(x, axis=-1, eps=1e-05):
    m = jnp.mean(x, axis=axis, keepdims=True)
    v = jnp.var(x, axis=axis, keepdims=True)
    return (x - m) / jnp.sqrt(v + eps)

def _scatter_add(tgt, idx, src, axis=0):
    return tgt.at[idx].add(src)

def _segment_sum(src, seg, n):
    return jax.ops.segment_sum(src, seg, n)
kernel_name = 'mk_xattn_ffn_d2_seqx_r4_0f458c'

def setup_inputs(seed: int=0):
    np.random.seed(seed)
    _w = jnp.asarray

    def _rec_inputs():
        import jax
        import jax.numpy as jnp
        _rk = jax.random.key(seed)
        x = -0.0005207 + 1.001 * jax.random.normal(jax.random.fold_in(_rk, 1), (16, 512, 256), jnp.float32)
        _lenS = 512 - jax.random.randint(jax.random.fold_in(_rk, 7), (16,), 0, max(1, 512 // 4) + 1, jnp.int32)
        _lenS2 = 1601 - jax.random.randint(jax.random.fold_in(_rk, 8), (16,), 0, max(1, 1601 // 4) + 1, jnp.int32)
        _ctx_1024P = jax.random.normal(jax.random.fold_in(_rk, 11), (16, 16, 256), jnp.float32)
        _ctx_1024c = jax.random.dirichlet(jax.random.fold_in(_rk, 511), 0.3 * jnp.ones((16,), jnp.float32), (16, 1601))
        _ctx_1024t = jnp.einsum('bsk,bkd->bsd', _ctx_1024c, _ctx_1024P)
        _ctx_1024t = _ctx_1024t * jax.lax.rsqrt(jnp.mean(jnp.square(_ctx_1024t)) + 1e-12) * 0.953939
        ctx_1024 = -0.000514642 + 1.00011 * (_ctx_1024t + 0.3 * jax.random.normal(jax.random.fold_in(_rk, 611), (16, 1601, 256), jnp.float32))
        _validS = jnp.arange(512)[None, :] < _lenS[:, None]
        _validS2 = jnp.arange(1601)[None, :] < _lenS2[:, None]
        _causal = jnp.tril(jnp.ones((512, 512), dtype=bool))
        mask_BxS2_if1 = jnp.where(jnp.ones((16, 1601), dtype=bool), 1, 0).astype(jnp.int32)
        return (x, ctx_1024, mask_BxS2_if1)
    x, ctx_1024, mask_BxS2_if1 = _rec_inputs()

    def _L0_xattn_setup():
        import jax, jax.numpy as jnp
        import numpy as np
        EMBED_DIM = 256
        NUM_HEADS = 16
        HEAD_DIM = EMBED_DIM // NUM_HEADS
        WINDOW = 64

        def apply_rope(x):
            B, H, S, d = x.shape
            half = d // 2
            pos = jnp.arange(S, dtype=x.dtype)
            freqs = 1.0 / 10000.0 ** (jnp.arange(half, dtype=x.dtype) / half)
            ang = pos[:, None] * freqs[None, :]
            cos, sin = (jnp.cos(ang), jnp.sin(ang))
            x1, x2 = (x[..., :half], x[..., half:])
            return jnp.concatenate([x1 * cos - x2 * sin, x1 * sin + x2 * cos], axis=-1)

        def _forward(query, key, value, q_w, q_b, k_w, k_b, v_w, v_b, o_w, o_b):
            B, S_q, D = query.shape
            S_k = key.shape[1]
            H, d, W = (NUM_HEADS, HEAD_DIM, WINDOW)
            q = (query @ q_w.T + q_b).reshape(B, S_q, H, d).transpose(0, 2, 1, 3)
            k = (key @ k_w.T + k_b).reshape(B, S_k, H, d).transpose(0, 2, 1, 3)
            v = (value @ v_w.T + v_b).reshape(B, S_k, H, d).transpose(0, 2, 1, 3)
            q = apply_rope(q) * d ** (-0.5)
            k = apply_rope(k)
            q_pos = jnp.arange(S_q)[:, None]
            offsets = jnp.arange(-W, 1)[None, :]
            idx = q_pos + offsets
            local_mask = (idx < 0) | (idx >= S_k)
            gidx = jnp.clip(idx, 0, S_k - 1)
            k_win = k[:, :, gidx, :]
            v_win = v[:, :, gidx, :]
            scores = jnp.einsum('bhqd,bhqwd->bhqw', q, k_win)
            mask = local_mask[None, None, :, :]
            scores = jnp.where(mask, -jnp.inf, scores)
            m = jnp.max(scores, axis=-1, keepdims=True)
            m = jnp.where(jnp.isfinite(m), m, 0.0)
            e = jnp.exp(scores - m)
            denom = jnp.sum(e, axis=-1, keepdims=True)
            probs = jnp.where(denom > 0, e / jnp.where(denom > 0, denom, 1.0), 0.0)
            ctx = jnp.einsum('bhqw,bhqwd->bhqd', probs, v_win)
            ctx = ctx.transpose(0, 2, 1, 3).reshape(B, S_q, D)
            return ctx @ o_w.T + o_b
        key = jax.random.key(seed)
        ks = jax.random.split(key, 12)
        B, S, D = (1, 512, EMBED_DIM)
        scale = 1.0 / np.sqrt(D)
        inp = {'query': jax.random.normal(ks[0], (B, S, D), jnp.float32), 'key': jax.random.normal(ks[1], (B, S, D), jnp.float32), 'value': jax.random.normal(ks[2], (B, S, D), jnp.float32), 'q_w': jax.random.normal(ks[3], (D, D), jnp.float32) * scale, 'q_b': jax.random.normal(ks[4], (D,), jnp.float32) * 0.01, 'k_w': jax.random.normal(ks[5], (D, D), jnp.float32) * scale, 'k_b': jax.random.normal(ks[6], (D,), jnp.float32) * 0.01, 'v_w': jax.random.normal(ks[7], (D, D), jnp.float32) * scale, 'v_b': jax.random.normal(ks[8], (D,), jnp.float32) * 0.01, 'o_w': jax.random.normal(ks[9], (D, D), jnp.float32) * scale, 'o_b': jax.random.normal(ks[10], (D,), jnp.float32) * 0.01}
        return inp
    _L0_xattn_all = _L0_xattn_setup()
    _L0_xattn_in = {k: v for k, v in _L0_xattn_all.items() if k in ('q_w', 'q_b', 'k_w', 'k_b', 'v_w', 'v_b', 'o_w', 'o_b')}
    del _L0_xattn_all

    def _L0_ffn_setup():
        import jax, jax.numpy as jnp
        import numpy as np
        from jax import lax
        T, B, I, M, O = (64, 64, 256, 256, 256)

        def _xavier(key, shape):
            fan_out, fan_in = shape
            limit = float(np.sqrt(6.0 / (fan_in + fan_out)))
            return jax.random.uniform(key, shape, jnp.float32, -limit, limit)
        key = jax.random.key(seed)
        ks = jax.random.split(key, 9)
        x = jax.random.normal(ks[0], (T, B, I), jnp.float32)
        return {'x': x, 'wf': _xavier(ks[1], (M, I)), 'uf': _xavier(ks[2], (M, M)), 'bf': jnp.zeros((M,), jnp.float32), 'wi': _xavier(ks[3], (M, I)), 'ui': _xavier(ks[4], (M, M)), 'bi': jnp.zeros((M,), jnp.float32), 'wc': _xavier(ks[5], (M, I)), 'uc': _xavier(ks[6], (M, M)), 'bc': jnp.zeros((M,), jnp.float32), 'wo': _xavier(ks[7], (O, I)), 'uo': _xavier(ks[8], (O, M)), 'bo': jnp.zeros((O,), jnp.float32), 'in_c': jnp.zeros((M,), jnp.float32)}
    _L0_ffn_all = _L0_ffn_setup()
    _L0_ffn_in = {k: v for k, v in _L0_ffn_all.items() if k in ('wf', 'uf', 'bf', 'wi', 'ui', 'bi', 'wc', 'uc', 'bc', 'wo', 'uo', 'bo', 'in_c')}
    del _L0_ffn_all

    def _L1_xattn_setup():
        import jax, jax.numpy as jnp
        import numpy as np
        D_MODEL = 256
        NUM_HEADS = 16
        D_K = D_MODEL // NUM_HEADS
        NEG_INF = -1000000000.0
        key = jax.random.key(seed)
        ks = jax.random.split(key, 12)
        B, S = (2, 512)
        scale = 1.0 / np.sqrt(D_MODEL)
        inp = {'q': jax.random.normal(ks[0], (B, S, D_MODEL), jnp.float32), 'k': jax.random.normal(ks[1], (B, S, D_MODEL), jnp.float32), 'v': jax.random.normal(ks[2], (B, S, D_MODEL), jnp.float32), 'mask': jnp.ones((B, S), jnp.int32), 'W_q': jax.random.normal(ks[3], (D_MODEL, D_MODEL), jnp.float32) * scale, 'b_q': jnp.zeros((D_MODEL,), jnp.float32), 'W_k': jax.random.normal(ks[4], (D_MODEL, D_MODEL), jnp.float32) * scale, 'b_k': jnp.zeros((D_MODEL,), jnp.float32), 'W_v': jax.random.normal(ks[5], (D_MODEL, D_MODEL), jnp.float32) * scale, 'b_v': jnp.zeros((D_MODEL,), jnp.float32), 'W_o': jax.random.normal(ks[6], (D_MODEL, D_MODEL), jnp.float32) * scale, 'b_o': jnp.zeros((D_MODEL,), jnp.float32)}
        return inp
    _L1_xattn_all = _L1_xattn_setup()
    _L1_xattn_in = {k: v for k, v in _L1_xattn_all.items() if k in ('W_q', 'b_q', 'W_k', 'b_k', 'W_v', 'b_v', 'W_o', 'b_o')}
    del _L1_xattn_all

    def _L1_ffn_setup():
        import jax, jax.numpy as jnp
        import numpy as np
        E = 8
        K = 2
        CAP_RATIO = 1.05
        key = jax.random.key(seed)
        ks = jax.random.split(key, 4)
        B, S, D, H = (2, 512, 256, 1024)
        x = jax.random.normal(ks[0], (B, S, D), jnp.float32)
        Wg = jax.random.normal(ks[1], (E, D), jnp.float32) * 0.02
        W1 = jax.random.normal(ks[2], (E, D, H), jnp.float32) * 0.02
        b1 = jnp.zeros((E, H), jnp.float32)
        W2 = jax.random.normal(ks[3], (E, H, D), jnp.float32) * 0.02
        b2 = jnp.zeros((E, D), jnp.float32)
        return {'x': x, 'Wg': Wg, 'W1': W1, 'b1': b1, 'W2': W2, 'b2': b2}
    _L1_ffn_all = _L1_ffn_setup()
    _L1_ffn_in = {k: v for k, v in _L1_ffn_all.items() if k in ('Wg', 'W1', 'b1', 'W2', 'b2')}
    del _L1_ffn_all
    return {'x': x, 'ctx_1024': ctx_1024, 'mask_BxS2_if1': mask_BxS2_if1, 'L0_xattn_q_w': _L0_xattn_in['q_w'], 'L0_xattn_q_b': _L0_xattn_in['q_b'], 'L0_xattn_k_w': _L0_xattn_in['k_w'], 'L0_xattn_k_b': _L0_xattn_in['k_b'], 'L0_xattn_v_w': _L0_xattn_in['v_w'], 'L0_xattn_v_b': _L0_xattn_in['v_b'], 'L0_xattn_o_w': _L0_xattn_in['o_w'], 'L0_xattn_o_b': _L0_xattn_in['o_b'], 'L0_ffn_wf': _L0_ffn_in['wf'], 'L0_ffn_uf': _L0_ffn_in['uf'], 'L0_ffn_bf': _L0_ffn_in['bf'], 'L0_ffn_wi': _L0_ffn_in['wi'], 'L0_ffn_ui': _L0_ffn_in['ui'], 'L0_ffn_bi': _L0_ffn_in['bi'], 'L0_ffn_wc': _L0_ffn_in['wc'], 'L0_ffn_uc': _L0_ffn_in['uc'], 'L0_ffn_bc': _L0_ffn_in['bc'], 'L0_ffn_wo': _L0_ffn_in['wo'], 'L0_ffn_uo': _L0_ffn_in['uo'], 'L0_ffn_bo': _L0_ffn_in['bo'], 'L0_ffn_in_c': _L0_ffn_in['in_c'], 'L1_xattn_W_q': _L1_xattn_in['W_q'], 'L1_xattn_b_q': _L1_xattn_in['b_q'], 'L1_xattn_W_k': _L1_xattn_in['W_k'], 'L1_xattn_b_k': _L1_xattn_in['b_k'], 'L1_xattn_W_v': _L1_xattn_in['W_v'], 'L1_xattn_b_v': _L1_xattn_in['b_v'], 'L1_xattn_W_o': _L1_xattn_in['W_o'], 'L1_xattn_b_o': _L1_xattn_in['b_o'], 'L1_ffn_Wg': _L1_ffn_in['Wg'], 'L1_ffn_W1': _L1_ffn_in['W1'], 'L1_ffn_b1': _L1_ffn_in['b1'], 'L1_ffn_W2': _L1_ffn_in['W2'], 'L1_ffn_b2': _L1_ffn_in['b2']}

def reference(x, ctx_1024, mask_BxS2_if1, L0_xattn_q_w, L0_xattn_q_b, L0_xattn_k_w, L0_xattn_k_b, L0_xattn_v_w, L0_xattn_v_b, L0_xattn_o_w, L0_xattn_o_b, L0_ffn_wf, L0_ffn_uf, L0_ffn_bf, L0_ffn_wi, L0_ffn_ui, L0_ffn_bi, L0_ffn_wc, L0_ffn_uc, L0_ffn_bc, L0_ffn_wo, L0_ffn_uo, L0_ffn_bo, L0_ffn_in_c, L1_xattn_W_q, L1_xattn_b_q, L1_xattn_W_k, L1_xattn_b_k, L1_xattn_W_v, L1_xattn_b_v, L1_xattn_W_o, L1_xattn_b_o, L1_ffn_Wg, L1_ffn_W1, L1_ffn_b1, L1_ffn_W2, L1_ffn_b2):
    import jax
    import jax.numpy as jnp

    def _L0_xattn_ref(query, key, value, q_w, q_b, k_w, k_b, v_w, v_b, o_w, o_b):
        import jax, jax.numpy as jnp
        import numpy as np
        EMBED_DIM = 256
        NUM_HEADS = 16
        HEAD_DIM = EMBED_DIM // NUM_HEADS
        WINDOW = 64

        def apply_rope(x):
            B, H, S, d = x.shape
            half = d // 2
            pos = jnp.arange(S, dtype=x.dtype)
            freqs = 1.0 / 10000.0 ** (jnp.arange(half, dtype=x.dtype) / half)
            ang = pos[:, None] * freqs[None, :]
            cos, sin = (jnp.cos(ang), jnp.sin(ang))
            x1, x2 = (x[..., :half], x[..., half:])
            return jnp.concatenate([x1 * cos - x2 * sin, x1 * sin + x2 * cos], axis=-1)

        def _forward(query, key, value, q_w, q_b, k_w, k_b, v_w, v_b, o_w, o_b):
            B, S_q, D = query.shape
            S_k = key.shape[1]
            H, d, W = (NUM_HEADS, HEAD_DIM, WINDOW)
            q = (query @ q_w.T + q_b).reshape(B, S_q, H, d).transpose(0, 2, 1, 3)
            k = (key @ k_w.T + k_b).reshape(B, S_k, H, d).transpose(0, 2, 1, 3)
            v = (value @ v_w.T + v_b).reshape(B, S_k, H, d).transpose(0, 2, 1, 3)
            q = apply_rope(q) * d ** (-0.5)
            k = apply_rope(k)
            q_pos = jnp.arange(S_q)[:, None]
            offsets = jnp.arange(-W, 1)[None, :]
            idx = q_pos + offsets
            local_mask = (idx < 0) | (idx >= S_k)
            gidx = jnp.clip(idx, 0, S_k - 1)
            k_win = k[:, :, gidx, :]
            v_win = v[:, :, gidx, :]
            scores = jnp.einsum('bhqd,bhqwd->bhqw', q, k_win)
            mask = local_mask[None, None, :, :]
            scores = jnp.where(mask, -jnp.inf, scores)
            m = jnp.max(scores, axis=-1, keepdims=True)
            m = jnp.where(jnp.isfinite(m), m, 0.0)
            e = jnp.exp(scores - m)
            denom = jnp.sum(e, axis=-1, keepdims=True)
            probs = jnp.where(denom > 0, e / jnp.where(denom > 0, denom, 1.0), 0.0)
            ctx = jnp.einsum('bhqw,bhqwd->bhqd', probs, v_win)
            ctx = ctx.transpose(0, 2, 1, 3).reshape(B, S_q, D)
            return ctx @ o_w.T + o_b
        return _forward(query, key, value, q_w, q_b, k_w, k_b, v_w, v_b, o_w, o_b)

    def _L0_ffn_ref(x, wf, uf, bf, wi, ui, bi, wc, uc, bc, wo, uo, bo, in_c):
        import jax, jax.numpy as jnp
        import numpy as np
        from jax import lax
        T, B, I, M, O = (64, 64, 256, 256, 256)

        def _xavier(key, shape):
            fan_out, fan_in = shape
            limit = float(np.sqrt(6.0 / (fan_in + fan_out)))
            return jax.random.uniform(key, shape, jnp.float32, -limit, limit)
        batch = x.shape[1]
        c0 = jnp.broadcast_to(in_c, (batch, in_c.shape[0]))

        def step(c, xt):
            ft = jax.nn.sigmoid(xt @ wf.T + c @ uf.T + bf)
            it = jax.nn.sigmoid(xt @ wi.T + c @ ui.T + bi)
            gt = jnp.tanh(xt @ wc.T + c @ uc.T + bc)
            c = ft * c + it * gt
            return (c, None)
        c_final, _ = lax.scan(step, c0, x)
        h = jnp.tanh(jnp.einsum('tbi,oi->tbo', x, wo) + c_final @ uo.T + bo)
        return h

    def _L1_xattn_ref(q, k, v, mask, W_q, b_q, W_k, b_k, W_v, b_v, W_o, b_o):
        import jax, jax.numpy as jnp
        import numpy as np
        D_MODEL = 256
        NUM_HEADS = 16
        D_K = D_MODEL // NUM_HEADS
        NEG_INF = -1000000000.0
        B, S, _ = q.shape

        def proj(x, W, b):
            y = x @ W.T + b
            return y.reshape(B, -1, NUM_HEADS, D_K).transpose(0, 2, 1, 3)
        qh = proj(q, W_q, b_q)
        kh = proj(k, W_k, b_k)
        vh = proj(v, W_v, b_v)
        scores = jnp.einsum('bhqd,bhkd->bhqk', qh, kh) / jnp.sqrt(jnp.float32(D_K))
        m = mask[:, None, None, :]
        scores = jnp.where(m == 0, jnp.float32(NEG_INF), scores)
        attn = jax.nn.softmax(scores, axis=-1)
        context = jnp.einsum('bhqk,bhkd->bhqd', attn, vh)
        context = context.transpose(0, 2, 1, 3).reshape(B, S, D_MODEL)
        return context @ W_o.T + b_o

    def _L1_ffn_ref(x, Wg, W1, b1, W2, b2):
        import jax, jax.numpy as jnp
        import numpy as np
        E = 8
        K = 2
        CAP_RATIO = 1.05
        B, S, D = x.shape
        T = B * S
        xf = x.reshape(T, D)
        gates = jax.nn.softmax(xf @ Wg.T, axis=-1)
        topw, topi = jax.lax.top_k(gates, K)
        C = int(round(K * T * CAP_RATIO / E))
        e_ord = topi.T.reshape(-1)
        tok_ord = jnp.tile(jnp.arange(T), K)
        oh = jax.nn.one_hot(e_ord, E, dtype=jnp.int32)
        cnt = jnp.take_along_axis(jnp.cumsum(oh, 0) - oh, e_ord[:, None], 1)[:, 0]
        within = cnt < C
        pos = jnp.where(within, cnt, C)
        x_disp = xf[tok_ord]
        buf = jnp.zeros((E, C + 1, D), xf.dtype).at[e_ord, pos].add(x_disp)[:, :C]
        h = jax.nn.gelu(jnp.einsum('ecd,edh->ech', buf, W1) + b1[:, None, :], approximate=False)
        y = jnp.einsum('ech,ehd->ecd', h, W2) + b2[:, None, :]
        y_ord = y[e_ord, jnp.minimum(pos, C - 1)] * within[:, None].astype(y.dtype)
        y_tk = y_ord.reshape(K, T, D).transpose(1, 0, 2)
        cw = topw * within.reshape(K, T).T.astype(topw.dtype)
        out = jnp.einsum('tk,tkd->td', cw, y_tk)
        return out.reshape(B, S, D)
    x = x + _L0_xattn_ref(_layernorm(x, axis=-1), ctx_1024, ctx_1024, L0_xattn_q_w, L0_xattn_q_b, L0_xattn_k_w, L0_xattn_k_b, L0_xattn_v_w, L0_xattn_v_b, L0_xattn_o_w, L0_xattn_o_b)
    x = x + _L0_ffn_ref(_layernorm(x, axis=-1), L0_ffn_wf, L0_ffn_uf, L0_ffn_bf, L0_ffn_wi, L0_ffn_ui, L0_ffn_bi, L0_ffn_wc, L0_ffn_uc, L0_ffn_bc, L0_ffn_wo, L0_ffn_uo, L0_ffn_bo, L0_ffn_in_c)
    x = x + _L1_xattn_ref(_layernorm(x, axis=-1), ctx_1024, ctx_1024, mask_BxS2_if1, L1_xattn_W_q, L1_xattn_b_q, L1_xattn_W_k, L1_xattn_b_k, L1_xattn_W_v, L1_xattn_b_v, L1_xattn_W_o, L1_xattn_b_o)
    x = x + _L1_ffn_ref(_layernorm(x, axis=-1), L1_ffn_Wg, L1_ffn_W1, L1_ffn_b1, L1_ffn_W2, L1_ffn_b2)
    return x

_drawn_inputs = setup_inputs


def setup_inputs(seed=0):
    import zlib

    import numpy as np

    out = dict(_drawn_inputs(seed))
    spreads = {'L0_ffn_bf': (0.0, 0.799),
     'L0_ffn_bi': (0.0, 0.787),
     'L0_ffn_bc': (0.0, 0.1),
     'L0_ffn_bo': (0.0, 0.1),
     'L0_ffn_in_c': (0.0, 0.8),
     'L1_xattn_b_q': (0.0, 0.528),
     'L1_xattn_b_k': (0.0, 0.8),
     'L1_xattn_b_v': (0.0, 0.1),
     'L1_xattn_b_o': (0.0, 0.1),
     'L1_ffn_b1': (0.0, 0.8),
     'L1_ffn_b2': (0.0, 0.461)}
    factors = {'L0_xattn_q_b': 8.0,
     'L0_xattn_k_b': 8.0,
     'L0_xattn_v_b': 6.321,
     'L0_xattn_o_b': 6.162,
     'L1_ffn_W1': 3.024,
     'L1_ffn_W2': 2.808}
    for name, (base, spread) in spreads.items():
        noise = np.random.default_rng([zlib.crc32(name.encode()), seed]).standard_normal(out[name].shape)
        drawn = base * np.exp(spread * noise) if base else spread * noise
        out[name] = jnp.asarray(drawn.astype(out[name].dtype))
    for name, factor in factors.items():
        out[name] = (out[name] * factor).astype(out[name].dtype)
    return out
```

```python
from contextlib import ExitStack

import numpy as np

import concourse.bass as bass
from concourse import mybir

ACT = mybir.ActivationFunctionType
ALU = mybir.AluOpType
AX = mybir.AxisListType.X
F32 = mybir.dt.float32
BF16 = mybir.dt.bfloat16
I32 = mybir.dt.int32
U32 = mybir.dt.uint32

P = 128
BATCH, SQ, SK, D = 16, 512, 1601, 256
HEADS, HD = 16, 16
GROUP = 4
NG = HEADS // GROUP
STEPS = BATCH * NG
WINDOW = 64
KC = D // P
QT = SQ // P
TOKENS = BATCH * SQ
TILES = TOKENS // P
PART = 3
TERM_ROWS = 6 * HD
KT = -(-SK // P)
K_LAST = SK - (KT - 1) * P
EXPERTS, TOPK, HID = 8, 2, 1024
CAPACITY = int(round(TOPK * TOKENS * 1.05 / EXPERTS))
SLOT_TILES = -(-CAPACITY // P)
SLOTS = SLOT_TILES * P
NO_SLOT = float(1 << 20)
EPS = 1e-5
SCALE = HD ** -0.5
MASKED = -float(2 ** 32)
OUTSIDE = -float(2 ** 32)

KEY_CHUNKS = [(a, min(a + 512, SK)) for a in range(0, SK, 512)]


class Space:

    semaphores = []

    def __init__(self, nc, ctx, stage):
        self.nc, self.ctx, self.stage = nc, ctx, stage

    def sb(self, name, shape, dt=F32):
        return self.ctx.enter_context(self.nc.sbuf_tensor(f"{self.stage}_{name}", shape, dt))

    def ps(self, name, shape, dt=F32):
        return self.ctx.enter_context(self.nc.psum_tensor(f"{self.stage}_{name}", shape, dt))

    def sem(self, name):
        made = self.nc.alloc_semaphore(f"{self.stage}_{name}")
        Space.semaphores.append(made)
        return made

    def sems(self, name, n):
        return [self.sem(f"{name}{i}") for i in range(n)]


class Ring:

    def __init__(self, jobs, banks):
        self.names = [j[0] for j in jobs]
        self.consumer = dict(jobs)
        self.banks = banks
        self.of = {name: k % banks for k, name in enumerate(self.names)}
        self.per = {c: sum(1 for _, x in jobs if x == c) for c in {x for _, x in jobs}}
        self.per_pass = len(jobs)

    def full(self, name, n):
        return n * self.per_pass + self.names.index(name) + 1

    def before(self, name, n):
        k = self.names.index(name)
        same = [i for i in range(self.per_pass) if i % self.banks == k % self.banks]
        earlier = [i for i in same if i < k]
        prev, back = (earlier[-1], 0) if earlier else (same[-1], 1)
        who = self.consumer[self.names[prev]]
        nth = sum(1 for i in range(prev + 1) if self.consumer[self.names[i]] == who)
        return who, (n + 1 - back) * self.per[who] + nth

    def freed(self, name, n):
        who = self.consumer[name]
        k = self.names.index(name)
        return (n + 1) * self.per[who] + sum(1 for x in self.names[:k + 1] if self.consumer[x] == who)


def at_least(eng, sem, value):
    if not (isinstance(value, int) and value <= 0):
        eng.wait_ge(sem, value)


def passes(eng, total, body):
    body(0, 0)
    body(1, 1)
    with eng.Fori(1, total // 2) as i:
        for par in range(2):
            body(i * 2 + par, par)


def passes_ahead(eng, total, early, late):
    early(0, 0)
    for n in range(2):
        early(n + 1, 1 - n)
        late(n, n)
    with eng.Fori(1, total // 2 - 1) as i:
        for par in range(2):
            early(i * 2 + par + 1, 1 - par)
            late(i * 2 + par, par)
    early(total - 1, 1)
    late(total - 2, 0)
    late(total - 1, 1)


def passes_two_ahead(eng, total, early, late):
    early(0, 0)
    early(1, 1)

    def one(n, par):
        parts = late(n, par)
        next(parts)
        early(n + 2, par)
        next(parts, None)
    for n in range(2):
        one(n, n)
    with eng.Fori(1, total // 2 - 1) as i:
        for par in range(2):
            one(i * 2 + par, par)
    for n in (total - 2, total - 1):
        for _ in late(n, n % 2):
            pass


def chain_link(eng, sem, base):
    count = [0]

    def link(ins):
        count[0] += 1
        ins.then_inc(sem, 1)
        eng.wait_ge(sem, base + count[0])
    return link, count


def project_context(nc, d):
    v_jobs = [(f"V{t}", "dve") for t in range((KT + 1) // 2)]
    jobs = ([(f"K{c}{k}", "dve") for c in range(KC) for k in range(4)]
            + [(f"T{c}", "act") for c in range(KC)] + v_jobs
            + [(f"R{u}{s}", "dve") for u in (0, 1) for s in "ab"]
            + [(f"W{t}", "dve") for t in range(2)]
            + [(f"R{u}{s}", "dve") for u in (2, 3) for s in "ab"])
    ring = Ring(jobs, 8)
    UNITS = 2 + 2 * KC
    LINKS = 3
    with ExitStack() as ctx:
        s = Space(nc, ctx, "ctxp")
        bank = [s.ps(f"bank{i}", [P, 512]) for i in range(8)]
        ctxT = [s.sb(f"ctxT{i}", [P, KC, SK]) for i in range(2)]
        x_in = [s.sb(f"x{i}", [P, QT, D]) for i in range(2)]
        mask_in = [s.sb(f"mask{i}", [P, SK], I32) for i in range(2)]
        w = {k: s.sb(k, [P, KC, D]) for k in ("wk1", "wv1", "wk0", "wk0p", "wv0", "wq0", "wq0p")}
        b = {k: s.sb(k, [P, KC]) for k in ("bk1", "bk0", "bk0p", "bq0", "bq0p")}
        bv1 = s.sb("bv1", [P, 2, D])
        bv0 = s.sb("bv0", [P, 2, D])
        cos, sin = s.sb("cos", [P, SQ]), s.sb("sin", [P, SQ])
        ident = s.sb("ident", [P, P])
        zero = s.sb("zero", [P, 2048])
        mask = s.sb("maskf", [P, SK])
        bias_row = s.sb("bias_row", [1, SK], BF16)
        whole1 = [s.sb(f"whole1{c}", [P, SK]) for c in range(KC)]
        rest1 = [s.sb(f"rest1{c}", [P, SK]) for c in range(KC)]
        parts1 = [s.sb(f"parts1{c}", [P, PART, SK], BF16) for c in range(KC)]
        wholeR = [s.sb(f"wholeR{u}", [P, SQ]) for u in range(4)]
        turned = [s.sb(f"turned{u}", [P, SQ]) for u in range(4)]
        restR = [s.sb(f"restR{u}", [P, SQ]) for u in range(4)]
        partsR = [s.sb(f"partsR{u}", [P, PART, SQ], BF16) for u in range(4)]
        whole, rest, parts = whole1 + wholeR, rest1 + restR, parts1 + partsR
        v1 = s.sb("v1", [P, KT, D])
        v0 = s.sb("v0", [P, QT, D])
        stats = s.sb("stats", [P, QT, 6])
        mv = s.sb("mv", [P, QT, 2])
        var_eps = s.sb("var_eps", [P, QT])
        minus_half = s.sb("minus_half", [P, QT])
        rstd = s.sb("rstd", [P, QT])
        xn = s.sb("xn", [P, QT, D])
        xnT = s.sb("xnT", [P, KC, SQ])

        const_in = s.sem("const_in")
        ctx_in, x_rd, mask_rd = s.sems("ctx_in", 2), s.sems("x_in", 2), s.sems("mask_in", 2)
        full = s.sem("full")
        free = {"dve": s.sem("free_dve"), "act": s.sem("free_act")}
        chain = s.sem("chain")
        zero_set, half_set = s.sem("zero_set"), s.sem("half_set")
        xbuf_zeroed = s.sem("xbuf_zeroed")
        stats_done = s.sem("stats_done")
        bias_done, var_done, rstd_done, xn_done = (
            s.sem("bias_done"), s.sem("var_done"), s.sem("rstd_done"), s.sem("xn_done"))
        whole_done, high_done, rest_done, mid_done, low_done = (
            s.sem("whole_done"), s.sem("high_done"), s.sem("rest_done"), s.sem("mid_done"),
            s.sem("low_done"))
        parts_out = s.sems("parts_out", UNITS)
        v1_out, v0_out, bias_out = s.sem("v1_out"), s.sem("v0_out"), s.sem("bias_out")
        CONSTS = 7 + 5 + 4 + 2 + 1

        block = ctx.enter_context(nc.Block())

        @block.sync
        def _(sp):
            for k, t in w.items():
                sp.dma_start(t[:, :, :], d[k].rearrange("(c p) n -> p c n", p=P)).then_inc(const_in, 16)
            for k, t in b.items():
                sp.dma_start(t[:, :], d[k]).then_inc(const_in, 16)
            for k, t in (("bv1", bv1), ("bv0", bv0)):
                for h in range(2):
                    sp.dma_start(t[:, h, :], d[k].partition_broadcast(P)).then_inc(const_in, 16)
            sp.dma_start(cos[:, :], d["cos"]).then_inc(const_in, 16)
            sp.dma_start(sin[:, :], d["sin"]).then_inc(const_in, 16)
            sp.dma_start(ident[:, :], d["ident"]).then_inc(const_in, 16)

            def loads(n, par):
                again = not (isinstance(n, int) and n < 2)
                if again:
                    sp.wait_ge(free["dve"], ring.freed("W1", n - 2))
                sp.dma_start(ctxT[par][:, :, :],
                             d["ctxT"][n].rearrange("(c p) k -> p c k", p=P)).then_inc(ctx_in[par], 16)
                sp.dma_start(x_in[par][:, :, :],
                             d["x"][n].rearrange("(i p) f -> p i f", p=P)).then_inc(x_rd[par], 16)
                sp.dma_start(mask_in[par][:, :], d["mask"][n].partition_broadcast(P)).then_inc(mask_rd[par], 16)

            def stores(n, par):
                sp.wait_ge(bias_done, n + 1)
                for g in range(NG):
                    sp.dma_start(d["bias1"][n * NG + g], bias_row[0:1, :]).then_inc(bias_out, 16)
                for u in range(2):
                    store_parts(n, u)
                sp.wait_ge(free["dve"], ring.freed("V6", n))
                for g in range(NG):
                    col = slice(g * 64, g * 64 + 64)
                    sp.dma_start(d["v1"][n * NG + g][0:(KT - 1) * P].rearrange("(t p) f -> p t f", p=P),
                                 v1[:, 0:KT - 1, col]).then_inc(v1_out, 16)
                    sp.dma_start(d["v1"][n * NG + g][(KT - 1) * P:SK],
                                 v1[0:K_LAST, KT - 1, col]).then_inc(v1_out, 16)
                for u in (2, 3):
                    store_parts(n, u)
                sp.wait_ge(free["dve"], ring.freed("W1", n))
                for g in range(NG):
                    sp.dma_start(d["v0"][n * NG + g].rearrange("(t p) f -> p t f", p=P),
                                 v0[:, :, g * 64:g * 64 + 64]).then_inc(v0_out, 16)
                for u in (4, 5):
                    store_parts(n, u)

            def store_parts(n, u):
                sp.wait_ge(low_done, UNITS * n + u + 1)
                name = "k1" if u < 2 else ("k0" if u < 4 else "q0")
                rows = d[name].rearrange("(b g) r (h k) -> b g (r h) k", g=NG, h=GROUP)[n]
                g = 2 * (u % 2)
                for part in range(PART):
                    sp.dma_start(rows[g:g + 2, 64 * part:64 * part + 64], parts[u][:, part, :]).then_inc(parts_out[u], 16)

            passes_ahead(sp, BATCH, loads, stores)
            for u in range(UNITS):
                sp.wait_ge(parts_out[u], 48 * BATCH)
            sp.wait_ge(v1_out, 128 * BATCH)
            sp.wait_ge(v0_out, 64 * BATCH)
            sp.wait_ge(bias_out, 64 * BATCH)

        @block.gpsimd
        def _(pool):
            nc.gpsimd.memset(minus_half[:, :], -0.5).then_inc(half_set, 1)
            nc.gpsimd.memset(zero[:, :], 0.0).then_inc(zero_set, 1)
            pool.wait_ge(zero_set, 1)
            pool.wait_ge(const_in, 16 * CONSTS)
            pool.wait_ge(ctx_in[0], 16)
            rows = d["xbuf"].rearrange("(p r) f -> p (r f)", p=P)
            for k in range(EXPERTS * SLOTS * D // P // 2048):
                pool.dma_start(rows[:, k * 2048:(k + 1) * 2048], zero[:, :]).then_inc(xbuf_zeroed, 16)
            pool.wait_ge(half_set, 1)

            def one(n, par):
                pool.wait_ge(var_done, n + 1)
                nc.gpsimd.tensor_tensor(rstd[:, :], var_eps[:, :], minus_half[:, :], ALU.pow).then_inc(rstd_done, 1)
                for u in range(UNITS):
                    pool.wait_ge(mid_done, UNITS * n + u + 1)
                    at_least(pool, parts_out[u], 48 * n)
                    nc.gpsimd.tensor_tensor(parts[u][:, 2, :], rest[u][:, :], parts[u][:, 1, :],
                                            ALU.subtract).then_inc(low_done, 1)
            passes(pool, BATCH, one)
            pool.wait_ge(xbuf_zeroed, 16 * (EXPERTS * SLOTS * D // P // 2048))

        @block.scalar
        def _(act):
            act.wait_ge(const_in, 16 * CONSTS)
            act.sem_inc(free["act"], ring.per["act"])

            def high(n, u):
                if u < 2:
                    act.wait_ge(free["dve"], ring.freed(f"K{u}3", n))
                else:
                    act.wait_ge(whole_done, 4 * n + u - 1)
                at_least(act, parts_out[u], 48 * n)
                nc.scalar.copy(parts[u][:, 0, :], whole[u][:, :]).then_inc(high_done, 1)

            def mid(n, u):
                act.wait_ge(rest_done, UNITS * n + u + 1)
                nc.scalar.copy(parts[u][:, 1, :], rest[u][:, :]).then_inc(mid_done, 1)

            def one(n, par):
                high(n, 0)
                high(n, 1)
                for c in range(KC):
                    act.wait_ge(full, ring.full(f"T{c}", n))
                    nc.scalar.copy(xnT[:, c, :], bank[ring.of[f"T{c}"]][:, :]).then_inc(free["act"], 1)
                mid(n, 0)
                mid(n, 1)
                for u in (2, 4):
                    high(n, u)
                    high(n, u + 1)
                    mid(n, u)
                    mid(n, u + 1)
            passes(act, BATCH, one)

        @block.vector
        def _(dve):
            dve.sem_inc(free["dve"], ring.per["dve"])
            dve.wait_ge(const_in, 16 * CONSTS)

            def rest_of(n, u):
                dve.wait_ge(high_done, UNITS * n + u + 1)
                if u < 2:
                    dve.wait_ge(free["dve"], ring.freed(f"K{u}3", n))
                else:
                    dve.wait_ge(whole_done, 4 * n + u - 1)
                at_least(dve, low_done, UNITS * n)
                nc.vector.tensor_tensor(rest[u][:, :], whole[u][:, :], parts[u][:, 0, :],
                                        ALU.subtract).then_inc(rest_done, 1)

            def one(n, par):
                link, count = chain_link(dve, chain, n * LINKS)
                dve.wait_ge(mask_rd[par], 8 * (n - par) + 16)
                link(nc.vector.tensor_scalar(mask[:, :], mask_in[par][:, :], 0.0, None, ALU.not_equal))
                at_least(dve, bias_out, 64 * n)
                nc.vector.tensor_scalar(bias_row[0:1, :], mask_in[par][0:1, :], 0.0, MASKED,
                                        ALU.is_equal, ALU.mult).then_inc(bias_done, 1)
                dve.wait_ge(x_rd[par], 8 * (n - par) + 16)
                for i in range(QT):
                    ins = nc.vector.bn_stats(stats[:, i, :], x_in[par][:, i, :])
                link(ins)
                dve.sem_inc(stats_done, 1)
                for i in range(QT):
                    ins = nc.vector.bn_aggr(mv[:, i, :], stats[:, i, :])
                link(ins)
                nc.vector.tensor_scalar(var_eps[:, :], mv[:, :, 1], EPS, None, ALU.add).then_inc(var_done, 1)
                dve.wait_ge(rstd_done, n + 1)
                for i in range(QT):
                    ins = nc.vector.tensor_scalar(xn[:, i, :], x_in[par][:, i, :], mv[:, i, 0:1],
                                                  rstd[:, i:i + 1], ALU.subtract, ALU.mult)
                ins.then_inc(xn_done, 1)
                for c in range(KC):
                    for k, (a, z) in enumerate(KEY_CHUNKS):
                        dve.wait_ge(full, ring.full(f"K{c}{k}", n))
                        nc.vector.scalar_tensor_tensor(
                            out=whole[c][:, a:z], in0=bank[ring.of[f"K{c}{k}"]][:, 0:z - a],
                            scalar=b["bk1"][:, c:c + 1], in1=mask[:, a:z],
                            op0=ALU.add, op1=ALU.mult).then_inc(free["dve"], 1)
                rest_of(n, 0)
                at_least(dve, v1_out, 128 * n)
                for t in range(7):
                    dve.wait_ge(full, ring.full(f"V{t}", n))
                    rows, two = (P, 2) if t < 6 else (K_LAST, 1)
                    ps = bank[ring.of[f"V{t}"]][0:rows, 0:two * D].rearrange("p (i f) -> p i f", i=two)
                    nc.vector.tensor_tensor(v1[0:rows, 2 * t:2 * t + two, :], ps, bv1[0:rows, 0:two, :],
                                            ALU.add).then_inc(free["dve"], 1)
                    if t == 3:
                        rest_of(n, 1)

                def turn(u):
                    kb, kp = ("bk0", "bk0p") if u < 2 else ("bq0", "bq0p")
                    c = u % 2
                    dve.wait_ge(full, ring.full(f"R{u}a", n))
                    nc.vector.scalar_tensor_tensor(
                        out=turned[u][:, :], in0=bank[ring.of[f"R{u}a"]][:, :], scalar=b[kb][:, c:c + 1],
                        in1=cos[:, :], op0=ALU.add, op1=ALU.mult).then_inc(free["dve"], 1)
                    dve.wait_ge(full, ring.full(f"R{u}b", n))
                    ins = nc.vector.scalar_tensor_tensor(
                        out=restR[u][:, :], in0=bank[ring.of[f"R{u}b"]][:, :], scalar=b[kp][:, c:c + 1],
                        in1=sin[:, :], op0=ALU.add, op1=ALU.mult)
                    ins.then_inc(free["dve"], 1)
                    dve.wait_ge(free["dve"], ring.freed(f"R{u}b", n))
                    nc.vector.tensor_tensor(wholeR[u][:, :], turned[u][:, :], restR[u][:, :],
                                            ALU.add).then_inc(whole_done, 1)

                at_least(dve, low_done, UNITS * n)
                turn(0)
                turn(1)
                rest_of(n, 2)
                rest_of(n, 3)
                at_least(dve, v0_out, 64 * n)
                for t in range(2):
                    dve.wait_ge(full, ring.full(f"W{t}", n))
                    ps = bank[ring.of[f"W{t}"]][:, :].rearrange("p (i f) -> p i f", i=2)
                    nc.vector.tensor_tensor(v0[:, 2 * t:2 * t + 2, :], ps, bv0[:, :, :],
                                            ALU.add).then_inc(free["dve"], 1)
                turn(2)
                turn(3)
                rest_of(n, 4)
                rest_of(n, 5)
                assert count[0] == LINKS
            passes(dve, BATCH, one)

        @block.tensor
        def _(pe):
            pe.wait_ge(const_in, 16 * CONSTS)

            def start_job(name, n):
                who, value = ring.before(name, n)
                pe.wait_ge(free[who], value)
                return bank[ring.of[name]]

            def feature_major(name, n, weights, c, moving):
                ps = start_job(name, n)
                cols = moving[0].shape[1]
                for kc in range(KC):
                    ins = nc.tensor.matmul(ps[:, 0:cols], weights[:, kc, c * P:(c + 1) * P], moving[kc],
                                           start=(kc == 0), stop=(kc == KC - 1))
                ins.then_inc(full, 1)
                return ins

            def token_major(name, n, par, tiles, weights):
                ps = start_job(name, n)
                for i, t in enumerate(tiles):
                    rows = min(P, SK - t * P)
                    for kc in range(KC):
                        ins = nc.tensor.matmul(ps[0:rows, i * D:(i + 1) * D],
                                               ctxT[par][:, kc, t * P:t * P + rows], weights[:, kc, :],
                                               start=(kc == 0), stop=(kc == KC - 1))
                ins.then_inc(full, 1)
                return ins

            def one(n, par):
                pe.wait_ge(ctx_in[par], 8 * (n - par) + 16)
                for c in range(KC):
                    for k, (a, z) in enumerate(KEY_CHUNKS):
                        feature_major(f"K{c}{k}", n, w["wk1"], c, [ctxT[par][:, kc, a:z] for kc in range(KC)])
                pe.wait_ge(xn_done, n + 1)
                for c in range(KC):
                    ps = start_job(f"T{c}", n)
                    for i in range(QT):
                        ins = nc.tensor.transpose(ps[:, i * P:(i + 1) * P], xn[:, i, c * P:(c + 1) * P], ident[:, :])
                    ins.then_inc(full, 1)
                for t in range(7):
                    token_major(f"V{t}", n, par, [2 * t, 2 * t + 1] if t < 6 else [12], w["wv1"])
                for u in (0, 1):
                    for side, ww in (("a", "wk0"), ("b", "wk0p")):
                        feature_major(f"R{u}{side}", n, w[ww], u, [ctxT[par][:, kc, 0:SQ] for kc in range(KC)])
                for t in range(2):
                    token_major(f"W{t}", n, par, [2 * t, 2 * t + 1], w["wv0"])
                pe.wait_ge(free["act"], ring.freed("T1", n))
                for u in (2, 3):
                    for side, ww in (("a", "wq0"), ("b", "wq0p")):
                        feature_major(f"R{u}{side}", n, w[ww], u - 2, [xnT[:, kc, :] for kc in range(KC)])
            passes(pe, BATCH, one)


class Step:

    def __init__(self, i, k):
        self.i, self.k = i, k
        self.n = i * 4 + k
        self.slot, self.par = k % 4, k % 2
        self.turn = i + k // 4

    def plus(self, m):
        return Step(self.i, self.k + m)


def windows(eng, body):
    for k in range(4):
        body(Step(0, k), k == 0, 2)
    with eng.Fori(1, STEPS // 4 - 1) as i:
        for k in range(4):
            body(Step(i, k), False, 2)
    for left in (3, 2, 1, 0):
        body(Step(0, STEPS - 1 - left), False, min(left, 2))


def window_attention(nc, d):
    attention(nc, d, "win", False)


def full_attention(nc, d):
    attention(nc, d, "full", True)


def attention(nc, d, stage, full):
    keys = SK if full else SQ
    kts = -(-keys // P)
    dk, dq, dv, dattn = (d[x + ("1" if full else "0")] for x in ("k", "q", "v", "attn"))
    SHIFT_ROW = TERM_ROWS + (1 if full else 0)
    ROWS = SHIFT_ROW + PART
    HQ = GROUP * QT
    SPAN = P + WINDOW
    LINKS = 4
    if full:
        PAIRS = (kts + 1) // 2
        MAXJOBS = [(h, [qt], c) for h in range(GROUP) for qt in range(QT) for c in range(3)]
        MAXJOBS = [j for h in range(GROUP) for j in [x for x in MAXJOBS if x[0] == h]
                   + ([(h, [0, 1, 2, 3], 3)] if h < 3 else [(h, [0, 1], 3), (h, [2, 3], 3)])]
        NCH, HEAD = 4, 16
    else:
        PAIRS = 1
        MAXJOBS = [(h, [qt, qt + 1], 0) for h in range(GROUP) for qt in (0, 2)]
        NCH, HEAD = 1, len(MAXJOBS)
    UNITS = PAIRS * GROUP
    NMAX = len(MAXJOBS)
    PER_WINDOW = NMAX + 1
    AHEAD = 6 if full else 2

    def window_items(s, left):
        items = []
        if left >= 1:
            items += [("max", s.plus(1), j) for j in range(HEAD, NMAX)]
        if left >= 2:
            items += [("max", s.plus(2), j) for j in range(AHEAD)]
        if left >= 1:
            items += [("turn", s.plus(1), 0)]
        if left >= 2:
            items += [("max", s.plus(2), j) for j in range(AHEAD, HEAD)]
        base = len(prologue) + PER_WINDOW * s.n
        at = len(prologue) + PER_WINDOW * (s.k % 3)
        return [(*it, base + n, (at + n) % 3) for n, it in enumerate(items)]

    def turn_number(s):
        if isinstance(s.n, int) and s.n == 0:
            return NMAX
        return len(prologue) + PER_WINDOW * (s.n - 1) + (NMAX - HEAD) + (AHEAD if not (isinstance(s.n, int) and s.n == STEPS - 1) else 0)

    prologue = ([("max", Step(0, 0), j) for j in range(NMAX)] + [("turn", Step(0, 0), 0)]
                + [("max", Step(0, 1), j) for j in range(HEAD)])
    prologue = [(*it, n, n % 3) for n, it in enumerate(prologue)]
    assert PER_WINDOW % 3 == 0

    with ExitStack() as ctx:
        sp_ = Space(nc, ctx, stage)
        sb, ps = sp_.sb, sp_.ps
        score = [ps(f"score{i}", [P, 2, 512]) for i in range(2)]
        item_bank = [ps(f"item{i}", [P, 512]) for i in range(3)]
        value = ps("value", [P, SQ])
        kst = [sb(f"kst{i}", [ROWS, GROUP, keys], BF16) for i in range(4)]
        qst = [sb(f"qst{i}", [ROWS, GROUP, SQ], BF16) for i in range(4)]
        vraw = [sb(f"vraw{i}", [P, kts, GROUP * HD]) for i in range(4)]
        vaug = [sb(f"vaug{i}", [P, kts, GROUP, 32]) for i in range(2)]
        cols = SQ if full else 2 * SPAN
        prob = [[sb(f"prob{h}{i}", [P, 2, cols]) for i in range(2)] for h in range(GROUP)]
        peak = [sb(f"peak{i}", [P, HQ, NCH]) for i in range(2)]
        shift = sb("shift", [P, HQ])
        shift_rest = sb("shift_rest", [P, HQ])
        shift_parts = sb("shift_parts", [P, P // HQ, HQ], BF16)
        shiftT = [sb(f"shiftT{i}", [P, P], BF16) for i in range(2)]
        raw = [sb(f"raw{i}", [P, SQ]) for i in range(2)]
        ident16 = sb("ident16", [P, P], BF16)
        outside = sb("outside", [P, 2, 2 * SPAN], BF16)

        sem, sems = sp_.sem, sp_.sems
        const_in, ones_set, pads_set, zeros_set = sem("const_in"), sem("ones_set"), sem("pads_set"), sem("zeros_set")
        stack_in, shift_in = sems("stack_in", 4), sems("shift_in", 4)
        score_full, exp_done, value_done, value_read = (
            sem("score_full"), sem("exp_done"), sem("value_done"), sem("value_read"))
        item_full, item_read = sem("item_full"), sem("item_read")
        chain, parts_done = sem("chain"), sem("parts_done")
        place_start, vaug_done = sem("place_start"), sem("vaug_done")
        attn_out = sems("attn_out", 2)
        STACK_DMAS = 3 + 3 + (1 if full else 0) + (2 if full else 1)

        def half(s):
            return (s.n - s.par) // 2 if isinstance(s.n, int) else s.i * 2 + (s.k - s.par) // 2

        block = ctx.enter_context(nc.Block())

        @block.sync
        def _(sp):
            sp.dma_start(ident16[:, :], d["ident16"]).then_inc(const_in, 16)
            sp.dma_start(outside[:, :, :], d["outside"]).then_inc(const_in, 16)
            for i in range(4):
                for t, width in ((kst[i], GROUP * keys), (qst[i], GROUP * SQ)):
                    sp.dma_start(t[TERM_ROWS:ROWS, :, :].rearrange("r h k -> r (h k)"),
                                 d["ones_rows"][0:ROWS - TERM_ROWS, 0:width]).then_inc(ones_set, 16)
            sp.wait_ge(ones_set, 128)

            def load(s):
                k, q, into = kst[s.slot], qst[s.slot], stack_in[s.slot]
                src, srq = dk[s.n], dq[s.n]
                at = 0
                for parts in (3, 2, 1):
                    rows = parts * HD
                    sp.dma_start(k[at:at + rows, :, :], src[0:rows].rearrange("r (h k) -> r h k", h=GROUP)).then_inc(into, 16)
                    at += rows
                at = 0
                for part, times in ((0, 3), (1, 2), (2, 1)):
                    rows = times * HD
                    sp.dma_start(q[at:at + rows, :, :].rearrange("r h k -> r (h k)"),
                                 srq[part * HD:(part + 1) * HD].unsqueeze(0).broadcast_to([times, HD, GROUP * SQ])).then_inc(into, 16)
                    at += rows
                if full:
                    sp.dma_start(k[TERM_ROWS:TERM_ROWS + 1, :, :],
                                 d["bias1"][s.n].unsqueeze(1).broadcast_to([1, GROUP, SK])).then_inc(into, 16)
                whole = keys // P
                sp.dma_start(vraw[s.slot][:, 0:whole, :],
                             dv[s.n][0:whole * P].rearrange("(t p) f -> p t f", p=P)).then_inc(into, 16)
                if full:
                    sp.dma_start(vraw[s.slot][0:K_LAST, KT - 1, :], dv[s.n][whole * P:SK]).then_inc(into, 16)

            def send_shift(s):
                sp.wait_ge(item_read, turn_number(s) + 1)
                sp.dma_start(qst[s.slot][SHIFT_ROW:ROWS, :, :].rearrange("o h (i q) -> o (h i) q", q=P),
                             shiftT[s.par][0:HQ * PART, :]).then_inc(shift_in[s.slot], 16)

            def store(s):
                sp.wait_ge(value_read, s.n + 1)
                sp.dma_start(dattn[s.n], raw[s.par][:, :]).then_inc(attn_out[s.par], 16)

            for k in range(3):
                load(Step(0, k))
            send_shift(Step(0, 0))

            def window(s, first, left):
                if first or not isinstance(s.n, int) or s.n + 3 < STEPS:
                    if not first:
                        sp.wait_ge(score_full, UNITS * s.n)
                        sp.wait_ge(vaug_done, s.n)
                    load(s.plus(3))
                if left >= 1 and not full:
                    send_shift(s.plus(1))
                if not first:
                    store(s.plus(-1))
                if left >= 1 and full:
                    send_shift(s.plus(1))
            windows(sp, window)
            store(Step(0, STEPS - 1))
            for i in range(2):
                sp.wait_ge(attn_out[i], 16 * STEPS // 2)

        @block.gpsimd
        def _(pool):
            for i in range(2):
                nc.gpsimd.memset(vaug[i][:, :, :, :], 0.0).then_inc(pads_set, 1)
                pool.wait_ge(pads_set, 2 * i + 1)
                nc.gpsimd.memset(vaug[i][:, :, :, HD:HD + 1], 1.0).then_inc(pads_set, 1)
            pool.wait_ge(pads_set, 4)

            def place_values(s):
                pool.wait_ge(stack_in[s.slot], 16 * STACK_DMAS * (s.turn + 1))
                pool.sem_inc(place_start, 1)
                for rows, a, z in ((P, 0, keys // P),) + (((K_LAST, KT - 1, KT),) if full else ()):
                    ins = nc.gpsimd.tensor_copy(vaug[s.par][0:rows, a:z, :, 0:HD],
                                                vraw[s.slot][0:rows, a:z, :].rearrange("p t (h f) -> p t h f", h=GROUP))
                ins.then_inc(vaug_done, 1)

            place_values(Step(0, 0))

            def window(s, first, left):
                if left >= 1:
                    at_least(pool, value_done, PAIRS * s.n)
                    place_values(s.plus(1))
            windows(pool, window)

        @block.scalar
        def _(act):
            def read_values(s):
                act.wait_ge(value_done, PAIRS * (s.n + 1))
                at_least(act, attn_out[s.par], 16 * half(s))
                nc.scalar.copy(raw[s.par][:, :], value[:, :]).then_inc(value_read, 1)

            def window(s, first, left):
                for t in range(PAIRS):
                    for h in range(GROUP):
                        u = t * GROUP + h
                        act.wait_ge(score_full, UNITS * s.n + u + 1)
                        at_least(act, value_done, PAIRS * s.n + t - 1)
                        rows, banks = (P, 2) if kts > 2 * t + 1 else (K_LAST, 1)
                        nc.scalar.activation(prob[h][(s.par * PAIRS + t) % 2][0:rows, 0:banks, :],
                                             score[u % 2][0:rows, 0:banks, 0:cols], ACT.Exp, scale=SCALE).then_inc(exp_done, 1)
                        if full and u == 4 and not first:
                            read_values(s.plus(-1))
                if not full and not first:
                    read_values(s.plus(-1))
            windows(act, window)
            read_values(Step(0, STEPS - 1))

        @block.vector
        def _(dve):
            nc.vector.memset(shift_parts[:, :, :], 0.0).then_inc(zeros_set, 1)
            dve.wait_ge(zeros_set, 1)
            dve.wait_ge(const_in, 32)

            def item(kind, s, j, number, bank):
                dve.wait_ge(item_full, number + 1)
                if kind == "turn":
                    if not (isinstance(s.n, int) and s.n < 2):
                        b = s.plus(-2)
                        dve.wait_ge(shift_in[b.slot], 16 * (b.turn + 1))
                    nc.vector.tensor_copy(shiftT[s.par][:, :], item_bank[bank][:, :].bitcast(BF16)[:, 0:P]).then_inc(item_read, 1)
                    return
                h, qts, c = MAXJOBS[j]
                hq, w = h * QT + qts[0], SPAN if not full else (512 if c < 3 else K_LAST)
                src = item_bank[bank][:, 0:len(qts) * w].rearrange("p (i k) -> p i k", k=w)
                nc.vector.tensor_reduce(peak[s.par][:, hq:hq + len(qts), c], src, AX, ALU.max).then_inc(item_read, 1)
                if j == NMAX - 1:
                    link, _ = chain_link(dve, chain, s.n * LINKS)
                    dve.wait_ge(item_read, number + 1)
                    link(nc.vector.tensor_reduce(shift[:, :], peak[s.par][:, :, :], AX, ALU.max, negate=True))
                    link(nc.vector.tensor_copy(shift_parts[:, 0, :], shift[:, :]))
                    link(nc.vector.tensor_tensor(shift_rest[:, :], shift[:, :], shift_parts[:, 0, :], ALU.subtract))
                    link(nc.vector.tensor_copy(shift_parts[:, 1, :], shift_rest[:, :]))
                    nc.vector.tensor_tensor(shift_parts[:, 2, :], shift_rest[:, :], shift_parts[:, 1, :],
                                            ALU.subtract).then_inc(parts_done, 1)

            for it in prologue:
                item(*it)

            def window(s, first, left):
                for it in window_items(s, left):
                    item(*it)
            windows(dve, window)

        @block.tensor
        def _(pe):
            pe.wait_ge(const_in, 32)

            def item(kind, s, j, number, bank):
                at_least(pe, item_read, number - 2)
                ps = item_bank[bank]
                if kind == "turn":
                    pe.wait_ge(parts_done, s.n + 1)
                    nc.tensor.transpose(ps[:, :].bitcast(BF16)[:, 0:P],
                                        shift_parts[:, :, :].rearrange("p a b -> p (a b)"), ident16[:, :]).then_inc(item_full, 1)
                    return
                if j == 0:
                    pe.wait_ge(stack_in[s.slot], 16 * STACK_DMAS * (s.turn + 1))
                h, qts, c = MAXJOBS[j]
                if not full:
                    nc.tensor.matmul(ps[:, 0:2 * SPAN], ident16[:, :], outside[:, 0 if qts[0] == 0 else 1, :],
                                     start=True, stop=True)
                for n, qt in enumerate(qts):
                    if full:
                        a, z = KEY_CHUNKS[c]
                        at = n * (z - a)
                    else:
                        a, z = max(0, qt * P - WINDOW), (qt + 1) * P
                        at = n * SPAN + SPAN - (z - a)
                    ins = nc.tensor.matmul(ps[:, at:at + z - a], qst[s.slot][0:SHIFT_ROW, h, qt * P:(qt + 1) * P],
                                           kst[s.slot][0:SHIFT_ROW, h, a:z], start=full, stop=True,
                                           skip_group_check=True)
                ins.then_inc(item_full, 1)

            def scores(s, t, h):
                u = t * GROUP + h
                at_least(pe, exp_done, UNITS * s.n + u - 1)
                ps = score[u % 2]
                if full:
                    for kt in range(2 * t, min(2 * t + 2, kts)):
                        a, z = kt * P, min(kt * P + P, SK)
                        ins = nc.tensor.matmul(ps[0:z - a, kt % 2, :], kst[s.slot][:, h, a:z], qst[s.slot][:, h, :],
                                               start=True, stop=True)
                else:
                    for kt in range(kts):
                        a, z = kt * P, min(kt * P + SPAN, SQ)
                        if kt % 2 == 0:
                            nc.tensor.matmul(ps[:, kt // 2, 0:2 * SPAN], ident16[:, :], outside[:, 1, :],
                                             start=True, stop=True)
                        at = kt % 2 * SPAN
                        ins = nc.tensor.matmul(ps[:, kt // 2, at:at + z - a], kst[s.slot][:, h, kt * P:(kt + 1) * P],
                                               qst[s.slot][:, h, a:z], start=False, stop=True, skip_group_check=True)
                ins.then_inc(score_full, 1)

            def values(s, kt):
                rows = min(P, keys - kt * P)
                if kt == 0:
                    pe.wait_ge(vaug_done, s.n + 1)
                    at_least(pe, value_read, s.n)
                if kt == 0 or (full and kt % 2 == 0):
                    pe.wait_ge(exp_done, UNITS * s.n + (GROUP * (kt // 2 + 1) if full else UNITS))
                for h in range(GROUP):
                    if full:
                        src = prob[h][(s.par * PAIRS + kt // 2) % 2][0:rows, kt % 2, :]
                        a, z = 0, SQ
                    else:
                        a, z = kt * P, min(kt * P + SPAN, SQ)
                        src = prob[h][s.par][:, kt // 2, kt % 2 * SPAN:kt % 2 * SPAN + z - a]
                    ins = nc.tensor.matmul(value[32 * h:32 * h + 32, a:z], vaug[s.par][0:rows, kt, h, :], src,
                                           start=(kt == 0), stop=(kt == kts - 1 or not full),
                                           skip_group_check=not full)
                if kt == kts - 1 or (full and kt % 2 == 1):
                    ins.then_inc(value_done, 1)

            def window_work(s, first):
                work = []
                for t in range(PAIRS):
                    for h in range(GROUP):
                        alone = t == 0 or (t, h) == (1, 0)
                        work += [(5 if alone else 3 if kts > 2 * t + 1 else 2, scores, s, t, h)]
                        if not full:
                            if not first:
                                work += [(1, values, s.plus(-1), h)]
                        elif t == 0:
                            if h % 2 == 0 and not first:
                                work += [(5, values, s.plus(-1), kts - 2 + h // 2)]
                        elif h % 2 == 1 and 2 * (t - 1) + h // 2 < kts - 2:
                            work += [(5, values, s, 2 * (t - 1) + h // 2)]
                return work

            for it in prologue:
                item(*it)

            def window(s, first, left):
                items = window_items(s, left)
                pe.wait_ge(shift_in[s.slot], 16 * (s.turn + 1))
                work = window_work(s, first)
                total, done, given = sum(w for w, *_ in work), 0, 0
                for weight, what, *where in work:
                    what(*where)
                    done += weight
                    due = len(items) * done // total
                    for it in items[given:due]:
                        item(*it)
                    given = due
            windows(pe, window)
            for kt in (range(kts - 2, kts) if full else range(kts)):
                values(Step(0, STEPS - 1), kt)


def centre_rows(nc, dve, t, x, xn, n, pass_sems):
    stats, mv, var_eps, rstd = t
    stats_done, mean_done, carry, var_done, rstd_done, xn_done = pass_sems
    for i in range(QT):
        ins = nc.vector.bn_stats(stats[:, i, :], x[:, i, :])
    ins.then_inc(stats_done, 1)
    dve.wait_ge(stats_done, n + 1)
    dve.sem_inc(carry, 1)
    for i in range(QT):
        ins = nc.vector.bn_aggr(mv[:, i, :], stats[:, i, :])
    ins.then_inc(mean_done, 1)
    dve.wait_ge(mean_done, n + 1)
    nc.vector.tensor_scalar(var_eps[:, :], mv[:, :, 1], EPS, None, ALU.add).then_inc(var_done, 1)
    dve.wait_ge(rstd_done, n + 1)
    for i in range(QT):
        ins = nc.vector.tensor_scalar(xn[:, i, :], x[:, i, :], mv[:, i, 0:1], rstd[:, i:i + 1],
                                      ALU.subtract, ALU.mult)
    ins.then_inc(xn_done, 1)


def norm_tensors(s):
    return (s.sb("stats", [P, QT, 6]), s.sb("mv", [P, QT, 2]), s.sb("var_eps", [P, QT]), s.sb("rstd", [P, QT]))


def norm_sems(s):
    return [s.sem(x) for x in ("stats_done", "mean_done", "carry", "var_done", "rstd_done", "xn_done")]


def close_window(nc, d):
    close_attention(nc, d, "cwin", False)


def close_full(nc, d):
    close_attention(nc, d, "cfull", True)


def close_attention(nc, d, stage, last):
    names = ("attn1", "x2", "x3", "wo1", "bo1") if last else ("attn0", "x", "x1", "wo0", "bo0")
    dattn, dres, dx, wo_d, bo_d = (d[k] for k in names)
    by_head = dattn.rearrange("s (h r) q -> (s h) r q", h=GROUP)
    dattn = dattn.rearrange("(b g) (h r) q -> b (g h) r q", g=NG, h=GROUP)
    with ExitStack() as ctx:
        s = Space(nc, ctx, stage)
        obank = [s.ps(f"obank{i}", [P, 2, D]) for i in range(4)]
        tbank = [s.ps(f"tbank{i}", [P, 512]) for i in range(2)]
        zbank = [s.ps(f"zbank{i}", [P, 2, D]) for i in range(2)]
        attn = [s.sb(f"attn{i}", [P, KC, SQ]) for i in range(2)]
        inv = [s.sb(f"inv{i}", [P, KC, SQ]) for i in range(2)]
        res = [s.sb(f"res{i}", [P, QT, D]) for i in range(2)]
        x = [s.sb(f"x{i}", [P, QT, D]) for i in range(2)]
        xn = [s.sb(f"xn{i}", [P, QT, D]) for i in range(2)]
        xT = [s.sb(f"xT{i}", [P, KC, SQ]) for i in range(2)]
        z = [s.sb(f"z{i}", [P, QT, EXPERTS if last else D]) for i in range(2)]
        wo = s.sb("wo", [P, KC, D])
        wz = s.sb("wz", [P, KC, EXPERTS if last else D])
        bo = s.sb("bo", [P, QT, D])
        below = s.sb("below", [P, BATCH * HEADS // P, SQ])
        ident = s.sb("ident", [P, P])
        minus_half = s.sb("minus_half", [P, QT])
        norm = norm_tensors(s)
        nsem = norm_sems(s)
        var_done, rstd_done, xn_done = nsem[3:]
        const_in, half_set = s.sem("const_in"), s.sem("half_set")
        loads_in, res_in = s.sems("loads_in", 2), s.sems("res_in", 2)
        below_in, inverted, inverse_out = s.sem("below_in"), s.sem("inverted"), s.sem("inverse_out")
        attn_ready, res_ready = s.sem("attn_ready"), s.sem("res_ready")
        o_full, o_read, t_full, t_read, z_full, z_read = (
            s.sem(k) for k in ("o_full", "o_read", "t_full", "t_read", "z_full", "z_read"))
        x_out, xT_out, xn_out, z_out = (s.sems(k, 2) for k in ("x_out", "xT_out", "xn_out", "z_out"))
        ZJOBS = 1 if last else 2

        def stored(eng, sem, n, par):
            if not (isinstance(n, int) and n < 2):
                eng.wait_ge(sem[par], 8 * (n - par))

        block = ctx.enter_context(nc.Block())

        @block.sync
        def _(sp):
            sp.dma_start(below[:, :, :], by_head[:, HD, :].rearrange("(p j) q -> p j q", p=P)).then_inc(below_in, 16)
            sp.dma_start(wo[:, :, :], wo_d.rearrange("(c p) n -> p c n", p=P)).then_inc(const_in, 16)
            sp.dma_start(wz[:, :, :], d["wg" if last else "rwo"].rearrange("(c p) n -> p c n", p=P)).then_inc(const_in, 16)
            sp.dma_start(ident[:, :], d["ident"]).then_inc(const_in, 16)
            for i in range(QT):
                sp.dma_start(bo[:, i, :], bo_d.partition_broadcast(P)).then_inc(const_in, 16)
            sp.wait_ge(inverted, 1)
            sp.dma_start(d["inverse"].rearrange("b h q -> (b h) q").rearrange("(p j) q -> p j q", p=P),
                         below[:, :, :]).then_inc(inverse_out, 16)
            sp.wait_ge(inverse_out, 16)

            def loads(n, par):
                sp.wait_ge(o_read, 2 * n + 2)
                for c in range(KC):
                    heads = dattn[n][8 * c:8 * c + 8]
                    sp.dma_start(inv[par][:, c, :], d["inverse"][n][8 * c:8 * c + 8].unsqueeze(1).broadcast_to([8, HD, SQ])).then_inc(loads_in[par], 16)
                    sp.dma_start(attn[par][:, c, :], heads[:, 0:HD, :]).then_inc(loads_in[par], 16)
                sp.dma_start(res[par][:, :, :], dres[n].rearrange("(i p) f -> p i f", p=P)).then_inc(res_in[par], 16)

            def stores(n, par):
                sp.wait_ge(o_read, 2 * n + 6)
                sp.dma_start(dx[n].rearrange("(i p) f -> p i f", p=P), x[par][:, :, :]).then_inc(x_out[par], 16)
                yield
                if not last:
                    sp.wait_ge(t_read, 2 * n + 4)
                    sp.dma_start(d["xn1T"][n].rearrange("(c p) q -> p c q", p=P), xT[par][:, :, :]).then_inc(xT_out[par], 16)
                    sp.wait_ge(z_read, 2 * n + 4)
                    sp.dma_start(d["z"][n].rearrange("(i p) f -> p i f", p=P), z[par][:, :, :]).then_inc(z_out[par], 16)
                else:
                    sp.wait_ge(xn_done, n + 1)
                    sp.dma_start(d["xn3"][n].rearrange("(i p) f -> p i f", p=P), xn[par][:, :, :]).then_inc(xn_out[par], 16)
                    sp.wait_ge(z_read, n + 3)
                    sp.dma_start(d["logits"][n], z[par][:, :, :].rearrange("p i e -> p (i e)")).then_inc(z_out[par], 16)
            passes_two_ahead(sp, BATCH, loads, stores)
            for i in range(2):
                sp.wait_ge(x_out[i], 8 * BATCH)
                sp.wait_ge(z_out[i], 8 * BATCH)
                sp.wait_ge((xn_out if last else xT_out)[i], 8 * BATCH)

        @block.gpsimd
        def _(pool):
            nc.gpsimd.memset(minus_half[:, :], -0.5).then_inc(half_set, 1)
            pool.wait_ge(half_set, 1)
            pool.wait_ge(const_in, 16 * 7)

            def early(n, par):
                pool.wait_ge(loads_in[par], 32 * (n - par) + 64)
                nc.gpsimd.tensor_tensor(attn[par][:, :, :], attn[par][:, :, :], inv[par][:, :, :], ALU.mult).then_inc(attn_ready, 1)
                pool.wait_ge(res_in[par], 8 * (n - par) + 16)
                nc.gpsimd.tensor_tensor(res[par][:, :, :], res[par][:, :, :], bo[:, :, :], ALU.add).then_inc(res_ready, 1)

            def late(n, par):
                pool.wait_ge(var_done, n + 1)
                nc.gpsimd.tensor_tensor(norm[3][:, :], norm[2][:, :], minus_half[:, :], ALU.pow).then_inc(rstd_done, 1)
            passes_ahead(pool, BATCH, early, late)

        @block.scalar
        def _(act):
            act.sem_inc(t_read, 2)
            act.sem_inc(z_read, 2)

            def one(n, par):
                for c in range(KC):
                    act.wait_ge(t_full, 2 * n + c + 1)
                    if c == 0 and not last:
                        stored(act, xT_out, n, par)
                    nc.scalar.copy(xT[par][:, c, :], tbank[c][:, :]).then_inc(t_read, 1)
                for j in range(ZJOBS):
                    act.wait_ge(z_full, ZJOBS * n + j + 1)
                    if j == 0:
                        stored(act, z_out, n, par)
                    if last:
                        src = zbank[par][:, :, :].rearrange("p i f -> p (i f)")[:, 0:QT * EXPERTS]
                        nc.scalar.copy(z[par][:, :, :], src.rearrange("p (i e) -> p i e", e=EXPERTS)).then_inc(z_read, 1)
                    else:
                        nc.scalar.copy(z[par][:, 2 * j:2 * j + 2, :], zbank[j][:, :, :]).then_inc(z_read, 1)
            passes(act, BATCH, one)

        @block.vector
        def _(dve):
            dve.sem_inc(o_read, 4)

            dve.wait_ge(below_in, 16)
            nc.vector.reciprocal(below[:, :, :], below[:, :, :]).then_inc(inverted, 1)

            def one(n, par):
                dve.wait_ge(res_ready, n + 1)
                stored(dve, x_out, n, par)
                for j in range(2):
                    dve.wait_ge(o_full, 2 * n + j + 1)
                    nc.vector.tensor_tensor(x[par][:, 2 * j:2 * j + 2, :], obank[2 * par + j][:, :, :],
                                            res[par][:, 2 * j:2 * j + 2, :], ALU.add).then_inc(o_read, 1)
                dve.wait_ge(o_read, 2 * n + 6)
                if last:
                    stored(dve, xn_out, n, par)
                centre_rows(nc, dve, norm, x[par], xn[par], n, nsem)
            passes(dve, BATCH, one)

        @block.tensor
        def _(pe):
            pe.wait_ge(const_in, 16 * 7)

            def project(n, par):
                pe.wait_ge(attn_ready, n + 1)
                for j in range(2):
                    pe.wait_ge(o_read, 2 * n + j + 1)
                    for i in range(2):
                        tile = slice((2 * j + i) * P, (2 * j + i + 1) * P)
                        for kc in range(KC):
                            ins = nc.tensor.matmul(obank[2 * par + j][:, i, :], attn[par][:, kc, tile], wo[:, kc, :],
                                                   start=(kc == 0), stop=(kc == KC - 1))
                    ins.then_inc(o_full, 1)

            def turn(n, par):
                pe.wait_ge(xn_done, n + 1)
                for c in range(KC):
                    pe.wait_ge(t_read, 2 * n + c + 1)
                    for i in range(QT):
                        ins = nc.tensor.transpose(tbank[c][:, i * P:(i + 1) * P], xn[par][:, i, c * P:(c + 1) * P], ident[:, :])
                    ins.then_inc(t_full, 1)
                pe.wait_ge(t_read, 2 * n + 4)
                for j in range(ZJOBS):
                    if last:
                        pe.wait_ge(z_read, n + 1)
                        bank = zbank[par][:, :, :].rearrange("p i f -> p (i f)")
                        outs = [bank[:, i * EXPERTS:(i + 1) * EXPERTS] for i in range(QT)]
                    else:
                        pe.wait_ge(z_read, 2 * n + j + 1)
                        outs = [zbank[j][:, i, :] for i in range(2)]
                    for i, o in enumerate(outs):
                        t = 2 * j + i
                        for kc in range(KC):
                            ins = nc.tensor.matmul(o, xT[par][:, kc, t * P:(t + 1) * P], wz[:, kc, :],
                                                   start=(kc == 0), stop=(kc == KC - 1))
                    ins.then_inc(z_full, 1)
            passes_ahead(pe, BATCH, project, turn)


def recurrence(nc, d):
    GATES = [(g, m) for m in range(KC) for g in "fic"]
    NGATE = len(GATES)
    with ExitStack() as ctx:
        s = Space(nc, ctx, "rec")
        bank = [s.ps(f"bank{i}", [P, SQ]) for i in range(NGATE)]
        cbank = [s.ps(f"cbank{i}", [P, 2, D]) for i in range(2)]
        w = {g: s.sb(f"w{g}", [P, KC, D]) for g in "fic"}
        u = {g: s.sb(f"u{g}", [P, KC, D]) for g in "fico"}
        b = {g: s.sb(f"b{g}", [P, KC]) for g in "fic"}
        bo = s.sb("bo", [P, 2, D])
        c0 = s.sb("c0", [P, KC])
        xT = [s.sb(f"xT{i}", [P, KC, SQ]) for i in range(2)]
        state = [s.sb(f"state{i}", [P, KC, SQ]) for i in range(2)]
        gate = {(g, m): s.sb(f"gate_{g}{m}", [P, SQ]) for g, m in GATES}
        kept = [s.sb(f"kept{m}", [P, SQ]) for m in range(KC)]
        new = [s.sb(f"new{m}", [P, SQ]) for m in range(KC)]
        cu = s.sb("cu", [P, QT, D])
        const_in, x_in = s.sem("const_in"), s.sems("x_in", 2)
        zero_set, state_done = s.sem("zero_set"), s.sem("state_done")
        gate_full, gate_done = s.sem("gate_full"), s.sem("gate_done")
        kept_done, new_done = s.sem("kept_done"), s.sem("new_done")
        cu_full, cu_done, cu_out = s.sem("cu_full"), s.sem("cu_done"), s.sem("cu_out")
        block = ctx.enter_context(nc.Block())
        CONSTS = 3 + 4 + 3 + 2 + 1

        @block.sync
        def _(sp):
            for g in "fic":
                sp.dma_start(w[g][:, :, :], d["rw" + g].rearrange("(c p) n -> p c n", p=P)).then_inc(const_in, 16)
                sp.dma_start(b[g][:, :], d["rb" + g]).then_inc(const_in, 16)
            for g in "fico":
                sp.dma_start(u[g][:, :, :], d["ru" + g].rearrange("(c p) n -> p c n", p=P)).then_inc(const_in, 16)
            for i in range(2):
                sp.dma_start(bo[:, i, :], d["rbo"].partition_broadcast(P)).then_inc(const_in, 16)
            sp.dma_start(c0[:, :], d["c0"]).then_inc(const_in, 16)

            def load(n, par):
                at_least(sp, gate_done, NGATE * n)
                sp.dma_start(xT[par][:, :, :], d["xn1T"][n].rearrange("(c p) q -> p c q", p=P)).then_inc(x_in[par], 16)
            passes(sp, BATCH, load)
            sp.wait_ge(cu_done, 2)
            sp.dma_start(d["cu"], cu[:, :, :].rearrange("p i f -> p (i f)")).then_inc(cu_out, 16)
            sp.wait_ge(cu_out, 16)

        @block.gpsimd
        def _(pool):
            def one(n, par):
                for m in range(KC):
                    pool.wait_ge(gate_done, NGATE * (n + 1) + 3 * m + 3)
                    nc.gpsimd.tensor_tensor(new[m][:, :], gate["i", m][:, :], gate["c", m][:, :], ALU.mult).then_inc(new_done, 1)
            passes(pool, BATCH, one)

        @block.scalar
        def _(act):
            act.wait_ge(const_in, 16 * CONSTS)
            act.sem_inc(gate_done, NGATE)

            def one(n, par):
                for k, (g, m) in enumerate(GATES):
                    act.wait_ge(gate_full, NGATE * n + k + 1)
                    nc.scalar.activation(gate[g, m][:, :], bank[k][:, :], ACT.Tanh if g == "c" else ACT.Sigmoid,
                                         bias=b[g][:, m:m + 1]).then_inc(gate_done, 1)
            passes(act, BATCH, one)

        @block.vector
        def _(dve):
            dve.wait_ge(const_in, 16 * CONSTS)
            nc.vector.memset(state[1][:, :, :], 0.0).then_inc(zero_set, 1)
            dve.wait_ge(zero_set, 1)
            for m in range(KC):
                nc.vector.tensor_scalar(state[0][:, m, :], state[1][:, m, :], c0[:, m:m + 1], None, ALU.add).then_inc(state_done, 1)

            def one(n, par):
                for m in range(KC):
                    dve.wait_ge(gate_done, NGATE * (n + 1) + 3 * m + 1)
                    dve.wait_ge(state_done, KC * n + m + 1)
                    nc.vector.tensor_tensor(kept[m][:, :], gate["f", m][:, :], state[par][:, m, :], ALU.mult).then_inc(kept_done, 1)
                    dve.wait_ge(kept_done, KC * n + m + 1)
                    dve.wait_ge(new_done, KC * n + m + 1)
                    nc.vector.tensor_tensor(state[1 - par][:, m, :], kept[m][:, :], new[m][:, :], ALU.add).then_inc(state_done, 1)
            passes(dve, BATCH, one)
            for j in range(2):
                dve.wait_ge(cu_full, j + 1)
                nc.vector.tensor_tensor(cu[:, 2 * j:2 * j + 2, :], cbank[j][:, :, :], bo[:, :, :], ALU.add).then_inc(cu_done, 1)

        @block.tensor
        def _(pe):
            pe.wait_ge(const_in, 16 * CONSTS)

            def one(n, par):
                pe.wait_ge(x_in[par], 8 * (n - par) + 16)
                for k, (g, m) in enumerate(GATES):
                    pe.wait_ge(gate_done, NGATE * n + k + 1)
                    for kc in range(KC):
                        nc.tensor.matmul(bank[k][:, :], w[g][:, kc, m * P:(m + 1) * P], xT[par][:, kc, :],
                                         start=(kc == 0), stop=False)
                pe.wait_ge(state_done, KC * (n + 1))
                for k, (g, m) in enumerate(GATES):
                    for kc in range(KC):
                        ins = nc.tensor.matmul(bank[k][:, :], u[g][:, kc, m * P:(m + 1) * P], state[par][:, kc, :],
                                               start=False, stop=(kc == KC - 1))
                    ins.then_inc(gate_full, 1)
            passes(pe, BATCH, one)
            pe.wait_ge(state_done, KC * (BATCH + 1))
            for j in range(2):
                for i in range(2):
                    t = 2 * j + i
                    for kc in range(KC):
                        ins = nc.tensor.matmul(cbank[j][:, i, :], state[0][:, kc, t * P:(t + 1) * P], u["o"][:, kc, :],
                                               start=(kc == 0), stop=(kc == KC - 1))
                ins.then_inc(cu_full, 1)


def open_full(nc, d):
    with ExitStack() as ctx:
        s = Space(nc, ctx, "open")
        tbank = [s.ps(f"tbank{i}", [P, 512]) for i in range(4)]
        qbank = [s.ps(f"qbank{i}", [P, 512]) for i in range(4)]
        z = [s.sb(f"z{i}", [P, QT, D]) for i in range(2)]
        x1 = [s.sb(f"x1{i}", [P, QT, D]) for i in range(2)]
        x2 = [s.sb(f"x2{i}", [P, QT, D]) for i in range(2)]
        h = [s.sb(f"h{i}", [P, QT, D]) for i in range(2)]
        xn = [s.sb(f"xn{i}", [P, QT, D]) for i in range(2)]
        xT = [s.sb(f"xT{i}", [P, KC, SQ]) for i in range(2)]
        cu = s.sb("cu", [P, QT, D])
        wq = s.sb("wq", [P, KC, D])
        bq = s.sb("bq", [P, KC])
        ident = s.sb("ident", [P, P])
        whole = [[s.sb(f"whole{i}{c}", [P, SQ]) for c in range(KC)] for i in range(2)]
        rest = [[s.sb(f"rest{i}{c}", [P, SQ]) for c in range(KC)] for i in range(2)]
        parts = [[s.sb(f"parts{i}{c}", [P, PART, SQ], BF16) for c in range(KC)] for i in range(2)]
        minus_half = s.sb("minus_half", [P, QT])
        norm = norm_tensors(s)
        nsem = norm_sems(s)
        var_done, rstd_done, xn_done = nsem[3:]
        const_in, half_set, loads_in = s.sem("const_in"), s.sem("half_set"), s.sems("loads_in", 2)
        pre_done, h_done, x2_done, t_full, t_read, q_full, q_read, high_done, rest_done, mid_done, low_done = (
            s.sem(k) for k in ("pre_done", "h_done", "x2_done", "t_full", "t_read", "q_full", "q_read",
                               "high_done", "rest_done", "mid_done", "low_done"))
        x2_out, parts_out = s.sems("x2_out", 2), s.sems("parts_out", 2)
        block = ctx.enter_context(nc.Block())

        def stored(eng, sem, n, par, per_pass=16):
            if not (isinstance(n, int) and n < 2):
                eng.wait_ge(sem[par], per_pass // 2 * (n - par))

        @block.sync
        def _(sp):
            sp.dma_start(cu[:, :, :].rearrange("p i f -> p (i f)"), d["cu"]).then_inc(const_in, 16)
            sp.dma_start(wq[:, :, :], d["wq1"].rearrange("(c p) n -> p c n", p=P)).then_inc(const_in, 16)
            sp.dma_start(bq[:, :], d["bq1"]).then_inc(const_in, 16)
            sp.dma_start(ident[:, :], d["ident"]).then_inc(const_in, 16)

            def loads(n, par):
                sp.wait_ge(x2_done, n + 1)
                sp.dma_start(z[par][:, :, :], d["z"][n].rearrange("(i p) f -> p i f", p=P)).then_inc(loads_in[par], 16)
                sp.dma_start(x1[par][:, :, :], d["x1"][n].rearrange("(i p) f -> p i f", p=P)).then_inc(loads_in[par], 16)

            def stores(n, par):
                sp.wait_ge(x2_done, n + 3)
                sp.dma_start(d["x2"][n].rearrange("(i p) f -> p i f", p=P), x2[par][:, :, :]).then_inc(x2_out[par], 16)
                yield
                for c in range(KC):
                    sp.wait_ge(low_done, KC * n + c + 1)
                    rows = d["q1"].rearrange("(b g) r (h k) -> b g (r h) k", g=NG, h=GROUP)[n]
                    for part in range(PART):
                        sp.dma_start(rows[2 * c:2 * c + 2, 64 * part:64 * part + 64], parts[par][c][:, part, :]).then_inc(parts_out[par], 16)
            passes_two_ahead(sp, BATCH, loads, stores)
            for i in range(2):
                sp.wait_ge(x2_out[i], 8 * BATCH)
                sp.wait_ge(parts_out[i], 48 * BATCH)

        @block.gpsimd
        def _(pool):
            nc.gpsimd.memset(minus_half[:, :], -0.5).then_inc(half_set, 1)
            pool.wait_ge(half_set, 1)
            pool.wait_ge(const_in, 64)

            def early(n, par):
                pool.wait_ge(loads_in[par], 32 + 16 * (n - par))
                nc.gpsimd.tensor_tensor(z[par][:, :, :], z[par][:, :, :], cu[:, :, :], ALU.add).then_inc(pre_done, 1)
                pool.wait_ge(var_done, n + 1)
                nc.gpsimd.tensor_tensor(norm[3][:, :], norm[2][:, :], minus_half[:, :], ALU.pow).then_inc(rstd_done, 1)

            def late(n, par):
                for c in range(KC):
                    pool.wait_ge(mid_done, KC * n + c + 1)
                    nc.gpsimd.tensor_tensor(parts[par][c][:, 2, :], rest[par][c][:, :], parts[par][c][:, 1, :],
                                            ALU.subtract).then_inc(low_done, 1)
            passes_ahead(pool, BATCH, early, late)

        @block.scalar
        def _(act):
            act.sem_inc(t_read, 4)

            def early(n, par):
                act.wait_ge(pre_done, n + 1)
                nc.scalar.activation(h[par][:, :, :], z[par][:, :, :], ACT.Tanh).then_inc(h_done, 1)

            def late(n, par):
                for c in range(KC):
                    act.wait_ge(t_full, 2 * n + c + 1)
                    nc.scalar.copy(xT[par][:, c, :], tbank[2 * par + c][:, :]).then_inc(t_read, 1)
                stored(act, parts_out, n, par, 96)
                for c in range(KC):
                    act.wait_ge(q_read, 2 * n + c + 5)
                    nc.scalar.copy(parts[par][c][:, 0, :], whole[par][c][:, :]).then_inc(high_done, 1)
                for c in range(KC):
                    act.wait_ge(rest_done, 2 * n + c + 1)
                    nc.scalar.copy(parts[par][c][:, 1, :], rest[par][c][:, :]).then_inc(mid_done, 1)
            passes_ahead(act, BATCH, early, late)

        @block.vector
        def _(dve):
            dve.sem_inc(x2_done, 2)
            dve.sem_inc(q_read, 4)
            dve.wait_ge(const_in, 64)

            def early(n, par):
                dve.wait_ge(h_done, n + 1)
                stored(dve, x2_out, n, par)
                nc.vector.tensor_tensor(x2[par][:, :, :], x1[par][:, :, :], h[par][:, :, :], ALU.add).then_inc(x2_done, 1)
                dve.wait_ge(x2_done, n + 3)
                centre_rows(nc, dve, norm, x2[par], xn[par], n, nsem)

            def late(n, par):
                for c in range(KC):
                    dve.wait_ge(q_full, 2 * n + c + 1)
                    nc.vector.tensor_scalar(whole[par][c][:, :], qbank[2 * par + c][:, :], bq[:, c:c + 1], None,
                                            ALU.add).then_inc(q_read, 1)
                for c in range(KC):
                    dve.wait_ge(high_done, 2 * n + c + 1)
                    dve.wait_ge(q_read, 2 * n + c + 5)
                    nc.vector.tensor_tensor(rest[par][c][:, :], whole[par][c][:, :], parts[par][c][:, 0, :],
                                            ALU.subtract).then_inc(rest_done, 1)
            passes_ahead(dve, BATCH, early, late)

        @block.tensor
        def _(pe):
            pe.wait_ge(const_in, 64)

            def one(n, par):
                pe.wait_ge(xn_done, n + 1)
                for c in range(KC):
                    pe.wait_ge(t_read, 2 * n + c + 1)
                    for i in range(QT):
                        ins = nc.tensor.transpose(tbank[2 * par + c][:, i * P:(i + 1) * P],
                                                  xn[par][:, i, c * P:(c + 1) * P], ident[:, :])
                    ins.then_inc(t_full, 1)
                pe.wait_ge(t_read, 2 * n + 6)
                for c in range(KC):
                    pe.wait_ge(q_read, 2 * n + c + 1)
                    for kc in range(KC):
                        ins = nc.tensor.matmul(qbank[2 * par + c][:, :], wq[:, kc, c * P:(c + 1) * P], xT[par][:, kc, :],
                                               start=(kc == 0), stop=(kc == KC - 1))
                    ins.then_inc(q_full, 1)
            passes(pe, BATCH, one)


def route(nc, d):
    CHOICES = TOPK * TILES
    with ExitStack() as ctx:
        s = Space(nc, ctx, "route")
        shape = [P, TILES, EXPERTS]
        both = [P, TOPK, TILES, EXPERTS]
        inside = s.ps("inside", [P, TOPK, TILES * EXPERTS])
        totals = s.ps("totals", [P, TOPK, TILES * EXPERTS])
        logit = s.sb("logit", shape)
        number = s.sb("number", shape)
        prefer = s.sb("prefer", shape)
        work = s.sb("work", shape)
        top = s.sb("top", [P, TOPK, TILES])
        best = s.sb("best", [P, TILES])
        chosen = s.sb("chosen", both)
        chosen16 = s.sb("chosen16", both, BF16)
        gate = s.sb("gate", shape)
        gsum = s.sb("gsum", [P, TILES])
        ginv = s.sb("ginv", [P, TILES])
        ones = s.sb("ones", [P, CHOICES])
        total = s.sb("total", both)
        upto = s.sb("upto", both)
        place = s.sb("place", both)
        pos = s.sb("pos", [P, TOPK, TILES])
        expert = s.sb("expert", [P, TOPK, TILES])
        within = s.sb("within", [P, TOPK, TILES])
        weight = s.sb("weight", [P, TOPK, TILES])
        weight_t = s.sb("weight_t", [P, TILES, TOPK])
        row = s.sb("row", [P, TOPK, TILES])
        row_u = s.sb("row_u", [P, TILES, TOPK], U32)
        to = s.sb("to", [P, TOPK, TILES])
        to_u = s.sb("to_u", [P, TILES, TOPK], U32)
        before = s.sb("before", [P, P], BF16)
        ones16 = s.sb("ones16", [P, P], BF16)
        xn = [s.sb(f"xn{i}", [P, QT, D]) for i in range(2)]
        index = [s.sb(f"index{i}", [P, QT * TOPK], U32) for i in range(2)]
        const_in, step = s.sem("const_in"), s.sem("step")
        sub_done, exp_done, chosen_done, counted = (s.sem(k) for k in ("sub_done", "exp_done", "chosen_done", "counted"))
        routed, stored = s.sem("routed"), s.sem("stored")
        xn_in, scattered, carry, index_done = s.sems("xn_in", 2), s.sems("scattered", 2), s.sem("carry"), s.sem("index_done")
        block = ctx.enter_context(nc.Block())

        @block.sync
        def _(sp):
            sp.dma_start(logit[:, :, :].rearrange("p (b i) e -> p b (i e)", i=QT),
                         d["logits"].rearrange("b p f -> p b f")).then_inc(const_in, 16)
            sp.dma_start(number[:, :, :].rearrange("p t e -> p (t e)"), d["expert_no"].partition_broadcast(P)).then_inc(const_in, 16)
            sp.dma_start(before[:, :], d["before"]).then_inc(const_in, 16)
            sp.dma_start(ones16[:, :], d["ones16"]).then_inc(const_in, 16)

            def load(n, par):
                if not (isinstance(n, int) and n < 2):
                    sp.wait_ge(scattered[par], 16 * QT * TOPK // 2 * (n - par))
                sp.dma_start(xn[par][:, :, :], d["xn3"][n].rearrange("(i p) f -> p i f", p=P)).then_inc(xn_in[par], 16)
            passes(sp, BATCH, load)
            sp.wait_ge(routed, 1)
            sp.dma_start(d["rows"], row_u[:, :, :].rearrange("p t k -> p (t k)")).then_inc(stored, 16)
            sp.dma_start(d["weights"], weight_t[:, :, :].rearrange("p t k -> p (t k)")).then_inc(stored, 16)
            sp.wait_ge(stored, 32)

        @block.gpsimd
        def _(pool):
            pool.wait_ge(routed, 1)

            def one(n, par):
                pool.wait_ge(xn_in[par], 8 * (n - par) + 16)
                at_least(pool, scattered[par], 16 * QT * TOPK // 2 * (n - par))
                pool.sem_inc(carry, 1)
                nc.gpsimd.tensor_copy(index[par][:, :],
                                      to_u[:, :, :].rearrange("p t k -> p (t k)")[:, bass.ds(n * (QT * TOPK), QT * TOPK)]
                                      ).then_inc(index_done, 1)
                pool.wait_ge(index_done, n + 1)
                pool.sem_inc(carry, 1)
                for i in range(QT):
                    for k in range(TOPK):
                        c = i * TOPK + k
                        pool.indirect_dma_start(d["xbuf"], bass.IndirectOffsetOnAxis(index[par][:, c:c + 1], 0),
                                                xn[par][:, i, :], None, bounds_check=EXPERTS * SLOTS - 1,
                                                oob_is_err=False).then_inc(scattered[par], 16)
            passes(pool, BATCH, one)
            for i in range(2):
                pool.wait_ge(scattered[i], 16 * QT * TOPK * BATCH // 2)

        @block.scalar
        def _(act):
            act.wait_ge(sub_done, 1)
            nc.scalar.activation(gate[:, :, :], gate[:, :, :], ACT.Exp).then_inc(exp_done, 1)

        @block.tensor
        def _(pe):
            pe.wait_ge(const_in, 64)
            pe.wait_ge(chosen_done, 1)
            for k in range(TOPK):
                rhs = chosen16[:, k, :, :].rearrange("p t e -> p (t e)")
                nc.tensor.matmul(inside[:, k, :], before[:, :], rhs, start=True, stop=True)
                ins = nc.tensor.matmul(totals[:, k, :], ones16[:, :], rhs, start=True, stop=True)
            ins.then_inc(counted, 1)

        @block.vector
        def _(dve):
            v = nc.vector
            dve.wait_ge(const_in, 64)
            link, _ = chain_link(dve, step, 0)
            wide = lambda t: t.unsqueeze(2).broadcast_to(shape)
            v.memset(ones[:, :], 1.0)
            link(v.tensor_scalar(prefer[:, :, :], number[:, :, :], -1.0, float(EXPERTS), ALU.mult, ALU.add))
            for k in range(TOPK):
                link(v.tensor_reduce(top[:, k, :], logit[:, :, :], AX, ALU.max))
                if k == 0:
                    v.tensor_tensor(gate[:, :, :], logit[:, :, :], wide(top[:, 0, :]), ALU.subtract).then_inc(sub_done, 1)
                link(v.tensor_tensor(work[:, :, :], logit[:, :, :], wide(top[:, k, :]), ALU.is_equal))
                link(v.tensor_tensor(work[:, :, :], work[:, :, :], prefer[:, :, :], ALU.mult))
                link(v.tensor_reduce(best[:, :], work[:, :, :], AX, ALU.max))
                link(v.tensor_tensor(chosen[:, k, :, :], work[:, :, :], wide(best[:, :]), ALU.is_equal))
                if k == 0:
                    link(v.scalar_tensor_tensor(out=logit[:, :, :], in0=chosen[:, 0, :, :], scalar=-1e30,
                                                in1=logit[:, :, :], op0=ALU.mult, op1=ALU.add))
            v.tensor_copy(chosen16[:, :, :, :], chosen[:, :, :, :]).then_inc(chosen_done, 1)
            dve.wait_ge(exp_done, 1)
            link(v.tensor_reduce(gsum[:, :], gate[:, :, :], AX, ALU.add))
            link(v.reciprocal(ginv[:, :], gsum[:, :]))
            for k in range(TOPK):
                link(v.tensor_tensor(work[:, :, :], gate[:, :, :], chosen[:, k, :, :], ALU.mult))
                link(v.tensor_reduce(weight[:, k, :], work[:, :, :], AX, ALU.add))
                link(v.tensor_tensor(weight[:, k, :], weight[:, k, :], ginv[:, :], ALU.mult))
            dve.wait_ge(counted, 1)
            link(v.tensor_copy(total[:, :, :, :].rearrange("p k t e -> p k (t e)"), totals[:, :, :]))
            tot, upt = (t[:, :, :, :].rearrange("p k t e -> p (k t) e") for t in (total, upto))
            for e in range(EXPERTS):
                ins = v.tensor_tensor_scan(upt[:, :, e], ones[:, :], tot[:, :, e], 0.0, ALU.mult, ALU.add)
            link(ins)
            link(v.tensor_tensor(place[:, :, :, :], upto[:, :, :, :], total[:, :, :, :], ALU.subtract))
            link(v.tensor_tensor(place[:, :, :, :].rearrange("p k t e -> p k (t e)"),
                                 place[:, :, :, :].rearrange("p k t e -> p k (t e)"), inside[:, :, :], ALU.add))
            link(v.tensor_tensor(place[:, :, :, :], place[:, :, :, :], chosen[:, :, :, :], ALU.mult))
            link(v.tensor_reduce(pos[:, :, :], place[:, :, :, :], AX, ALU.add))
            for k in range(TOPK):
                link(v.tensor_tensor(place[:, k, :, :], chosen[:, k, :, :], number[:, :, :], ALU.mult))
            link(v.tensor_reduce(expert[:, :, :], place[:, :, :, :], AX, ALU.add))
            link(v.tensor_scalar(within[:, :, :], pos[:, :, :], float(CAPACITY), None, ALU.is_lt))
            link(v.tensor_scalar(pos[:, :, :], pos[:, :, :], float(CAPACITY - 1), None, ALU.min))
            link(v.scalar_tensor_tensor(out=row[:, :, :], in0=expert[:, :, :], scalar=float(SLOTS), in1=pos[:, :, :],
                                        op0=ALU.mult, op1=ALU.add))
            link(v.tensor_tensor(weight[:, :, :], weight[:, :, :], within[:, :, :], ALU.mult))
            link(v.tensor_scalar(within[:, :, :], within[:, :, :], -NO_SLOT, NO_SLOT, ALU.mult, ALU.add))
            link(v.tensor_tensor(to[:, :, :], row[:, :, :], within[:, :, :], ALU.add))
            turned = "p k t -> p t k"
            link(v.tensor_copy(row_u[:, :, :], row[:, :, :].rearrange(turned)))
            link(v.tensor_copy(weight_t[:, :, :], weight[:, :, :].rearrange(turned)))
            v.tensor_copy(to_u[:, :, :], to[:, :, :].rearrange(turned)).then_inc(routed, 1)


def experts(nc, d):
    CHUNKS = [(a, min(a + QT, SLOT_TILES)) for a in range(0, SLOT_TILES, QT)]
    NC = len(CHUNKS)
    HC = HID // P
    YJOBS = [(c, j) for c, (a, z) in enumerate(CHUNKS) for j in range(-(-(z - a) // 2))]
    NY = len(YJOBS)
    rows_d = lambda t, n, c: d[t].rearrange("(e r) f -> e r f", e=EXPERTS)[n][CHUNKS[c][0] * P:CHUNKS[c][1] * P].rearrange("(i p) f -> p i f", p=P)
    assert NC % 2 == 1
    with ExitStack() as ctx:
        s = Space(nc, ctx, "moe")
        tbank = [s.ps(f"tbank{i}", [P, 512]) for i in range(2)]
        hbank = [s.ps(f"hbank{i}", [P, 512]) for i in range(4)]
        ybank = [s.ps(f"ybank{i}", [P, 2, D]) for i in range(2)]
        w1 = [s.sb(f"w1{i}", [P, KC, HID]) for i in range(2)]
        w2 = [s.sb(f"w2{i}", [P, HC, D]) for i in range(2)]
        b1 = [s.sb(f"b1{i}", [P, HC]) for i in range(2)]
        b2 = [s.sb(f"b2{i}", [P, 2, D]) for i in range(2)]
        x = [s.sb(f"x{i}", [P, QT, D]) for i in range(2)]
        xT = [s.sb(f"xT{i}", [P, KC, SQ]) for i in range(2)]
        hT = [s.sb(f"hT{i}", [P, HC, SQ]) for i in range(2)]
        y = [s.sb(f"y{i}", [P, QT, D]) for i in range(2)]
        ident = s.sb("ident", [P, P])
        const_in, w_in, x_in = s.sem("const_in"), s.sems("w_in", 2), s.sems("x_in", 2)
        t_full, t_read, h_full, h_read, y_full, y_read = (
            s.sem(k) for k in ("t_full", "t_read", "h_full", "h_read", "y_full", "y_read"))
        y_out = s.sems("y_out", 2)
        carry = s.sem("carry")
        block = ctx.enter_context(nc.Block())

        def parity(par, c):
            return (par + c) % 2

        def before(n, par, c):
            return (n * NC + (c - parity(par, c))) * 8

        def expert_passes(eng, body):
            body(0, 0, False)
            body(1, 1, False)
            with eng.Fori(1, EXPERTS // 2 - 1) as i:
                for par in range(2):
                    body(i * 2 + par, par, False)
            body(EXPERTS - 2, 0, False)
            body(EXPERTS - 1, 1, True)

        def following(n, par, c):
            return (n, par, c + 1) if c + 1 < NC else (n + 1, 1 - par, 0)

        @block.sync
        def _(sp):
            sp.dma_start(ident[:, :], d["ident"]).then_inc(const_in, 16)

            def load_weights(n, par):
                sp.wait_ge(y_read, NY * n + NY)
                sp.sem_inc(carry, 1)
                sp.dma_start(w1[par][:, :, :], d["w1"][n].rearrange("(c p) h -> p c h", p=P)).then_inc(w_in[par], 16)
                sp.dma_start(w2[par][:, :, :], d["w2"][n].rearrange("(c p) f -> p c f", p=P)).then_inc(w_in[par], 16)
                sp.dma_start(b1[par][:, :], d["b1"][n]).then_inc(w_in[par], 16)
                for i in range(2):
                    sp.dma_start(b2[par][:, i, :], d["b2"][n].partition_broadcast(P)).then_inc(w_in[par], 16)

            def load_rows(n, par, c):
                pg = parity(par, c)
                tiles = CHUNKS[c][1] - CHUNKS[c][0]
                if not (isinstance(n, int) and n == 0 and c < 2):
                    sp.wait_ge(t_full, (n * NC + (c - 1)) * 2)
                    sp.sem_inc(carry, 1)
                sp.dma_start(x[pg][:, 0:tiles, :], rows_d("xbuf", n, c)).then_inc(x_in[pg], 16)

            load_rows(0, 0, 0)
            load_weights(0, 0)

            def one(n, par, last):
                for c, (a, z) in enumerate(CHUNKS):
                    if not (last and c == NC - 1):
                        load_rows(*following(n, par, c))
                    if c == 0 and not last:
                        load_weights(n + 1, 1 - par)
                    pg = parity(par, c)
                    jobs = [k for k, (cc, _) in enumerate(YJOBS) if cc == c]
                    sp.wait_ge(y_read, NY * n + 2 * NY + jobs[-1] + 1)
                    sp.sem_inc(carry, 1)
                    sp.dma_start(rows_d("ybuf", n, c), y[pg][:, 0:z - a, :]).then_inc(y_out[pg], 16)
            expert_passes(sp, one)
            for i in range(2):
                sp.wait_ge(y_out[i], 16 * EXPERTS * NC // 2)

        @block.scalar
        def _(act):
            act.sem_inc(h_read, 4)

            def one(n, par, last):
                act.wait_ge(w_in[par], 40 * (n - par) + 80)
                for c, (a, z) in enumerate(CHUNKS):
                    cols = (z - a) * P
                    for k in range(HC):
                        act.wait_ge(h_full, (n * NC + c) * HC + k + 1)
                        nc.scalar.activation(hT[parity(par, c)][:, k, 0:cols], hbank[k % 4][:, 0:cols], ACT.Gelu,
                                             bias=b1[par][:, k:k + 1]).then_inc(h_read, 1)
            expert_passes(act, one)

        @block.vector
        def _(dve):
            dve.sem_inc(y_read, 2 * NY)

            def read_turned(n, par, c):
                cols = (CHUNKS[c][1] - CHUNKS[c][0]) * P
                for kc in range(KC):
                    dve.wait_ge(t_full, (n * NC + c) * 2 + kc + 1)
                    nc.vector.tensor_copy(xT[parity(par, c)][:, kc, 0:cols], tbank[kc][:, 0:cols]).then_inc(t_read, 1)

            read_turned(0, 0, 0)

            def one(n, par, last):
                dve.wait_ge(w_in[par], 40 * (n - par) + 80)
                for c, (a, z) in enumerate(CHUNKS):
                    if not (last and c == NC - 1):
                        read_turned(*following(n, par, c))
                    pg = parity(par, c)
                    at_least(dve, y_out[pg], before(n, par, c))
                    for k, (cc, j) in enumerate(YJOBS):
                        if cc == c:
                            two = min(2, z - a - 2 * j)
                            dve.wait_ge(y_full, NY * n + k + 1)
                            nc.vector.tensor_tensor(y[pg][:, 2 * j:2 * j + two, :], ybank[(par + k) % 2][:, 0:two, :],
                                                    b2[par][:, 0:two, :], ALU.add).then_inc(y_read, 1)
            expert_passes(dve, one)

        @block.tensor
        def _(pe):
            pe.wait_ge(const_in, 16)

            def turn(n, par, c):
                pg = parity(par, c)
                pe.wait_ge(x_in[pg], before(n, par, c) + 16)
                for kc in range(KC):
                    if not (isinstance(n, int) and n == 0 and c == 0):
                        pe.wait_ge(t_read, (n * NC + (c - 1)) * 2 + kc + 1)
                    for i in range(CHUNKS[c][1] - CHUNKS[c][0]):
                        ins = nc.tensor.transpose(tbank[kc][:, i * P:(i + 1) * P], x[pg][:, i, kc * P:(kc + 1) * P], ident[:, :])
                    ins.then_inc(t_full, 1)

            turn(0, 0, 0)

            def one(n, par, last):
                pe.wait_ge(w_in[par], 40 * (n - par) + 80)
                for c, (a, z) in enumerate(CHUNKS):
                    pg, cols = parity(par, c), (z - a) * P
                    pe.wait_ge(t_read, (n * NC + c) * 2 + 2)
                    for k in range(HC):
                        pe.wait_ge(h_read, (n * NC + c) * HC + k + 1)
                        for kc in range(KC):
                            ins = nc.tensor.matmul(hbank[k % 4][:, 0:cols], w1[par][:, kc, k * P:(k + 1) * P],
                                                   xT[pg][:, kc, 0:cols], start=(kc == 0), stop=(kc == KC - 1))
                        ins.then_inc(h_full, 1)
                    if not (last and c == NC - 1):
                        turn(*following(n, par, c))
                    pe.wait_ge(h_read, (n * NC + c) * HC + HC + 4)
                    for k, (cc, j) in enumerate(YJOBS):
                        if cc != c:
                            continue
                        pe.wait_ge(y_read, NY * n + k + 2 * NY - 1)
                        for i in range(2 * j, min(2 * j + 2, z - a)):
                            for hc in range(HC):
                                ins = nc.tensor.matmul(ybank[(par + k) % 2][:, i % 2, :], hT[pg][:, hc, i * P:(i + 1) * P],
                                                       w2[par][:, hc, :], start=(hc == 0), stop=(hc == HC - 1))
                        ins.then_inc(y_full, 1)
            expert_passes(pe, one)


def combine(nc, d):
    C = QT * TOPK
    with ExitStack() as ctx:
        s = Space(nc, ctx, "comb")
        rows = s.sb("rows", [P, TILES * TOPK], U32)
        weights = s.sb("weights", [P, TILES * TOPK])
        index = [s.sb(f"index{i}", [P, C], U32) for i in range(2)]
        weight = [s.sb(f"weight{i}", [P, C]) for i in range(2)]
        x3 = [s.sb(f"x3{i}", [P, QT, D]) for i in range(2)]
        y = [s.sb(f"y{i}", [P, C, D]) for i in range(2)]
        half = s.sb("half", [P, QT, D])
        out = [s.sb(f"out{i}", [P, QT, D]) for i in range(2)]
        const_in, x3_in, gathered, out_done = s.sem("const_in"), s.sems("x3_in", 2), s.sems("gathered", 2), s.sems("out_done", 2)
        carry, index_done, weight_done, half_done, added = (
            s.sem(k) for k in ("carry", "index_done", "weight_done", "half_done", "added"))
        block = ctx.enter_context(nc.Block())

        @block.sync
        def _(sp):
            sp.dma_start(rows[:, :], d["rows"]).then_inc(const_in, 16)
            sp.dma_start(weights[:, :], d["weights"]).then_inc(const_in, 16)

            def load(n, par):
                sp.wait_ge(added, n + 1)
                sp.dma_start(x3[par][:, :, :], d["x3"][n].rearrange("(i p) f -> p i f", p=P)).then_inc(x3_in[par], 16)

            def store(n, par):
                sp.wait_ge(added, n + 3)
                sp.dma_start(d["out"][n].rearrange("(i p) f -> p i f", p=P), out[par][:, :, :]).then_inc(out_done[par], 16)
            passes_ahead(sp, BATCH, load, store)
            for i in range(2):
                sp.wait_ge(out_done[i], 8 * BATCH)

        @block.gpsimd
        def _(pool):
            pool.wait_ge(const_in, 32)

            def one(n, par):
                pool.wait_ge(added, n + 1)
                pool.sem_inc(carry, 1)
                nc.gpsimd.tensor_copy(index[par][:, :], rows[:, bass.ds(n * C, C)]).then_inc(index_done, 1)
                pool.wait_ge(index_done, n + 1)
                pool.sem_inc(carry, 1)
                for c in range(C):
                    pool.indirect_dma_start(y[par][:, c, :], None, d["ybuf"],
                                            bass.IndirectOffsetOnAxis(index[par][:, c:c + 1], 0)).then_inc(gathered[par], 16)
            passes(pool, BATCH, one)

        @block.vector
        def _(dve):
            dve.sem_inc(added, 2)
            dve.wait_ge(const_in, 32)

            def one(n, par):
                nc.vector.tensor_copy(weight[par][:, :], weights[:, bass.ds(n * C, C)]).then_inc(weight_done, 1)
                dve.wait_ge(weight_done, n + 1)
                dve.wait_ge(x3_in[par], 8 * (n - par) + 16)
                dve.wait_ge(gathered[par], 16 * C // 2 * (n - par) + 16 * C)
                for i in range(QT):
                    ins = nc.vector.scalar_tensor_tensor(
                        out=half[:, i, :], in0=y[par][:, 2 * i, :], scalar=weight[par][:, 2 * i:2 * i + 1],
                        in1=x3[par][:, i, :], op0=ALU.mult, op1=ALU.add)
                ins.then_inc(half_done, 1)
                dve.wait_ge(half_done, n + 1)
                at_least(dve, out_done[par], 8 * (n - par))
                for i in range(QT):
                    ins = nc.vector.scalar_tensor_tensor(
                        out=out[par][:, i, :], in0=y[par][:, 2 * i + 1, :], scalar=weight[par][:, 2 * i + 1:2 * i + 2],
                        in1=half[:, i, :], op0=ALU.mult, op1=ALU.add)
                ins.then_inc(added, 1)
            passes(dve, BATCH, one)


ORDER = [16 * (4 * g + h) + f for g in range(NG) for f in range(HD) for h in range(GROUP)]
PARTNER = [16 * (4 * g + h) + (f + 8) % HD for g in range(NG) for f in range(HD) for h in range(GROUP)]


def shape_constants():
    half = HD // 2
    freqs = (np.float32(1.0) / np.float32(10000.0) ** (np.arange(half, dtype=np.float32) / np.float32(half))).astype(np.float32)
    ang = np.arange(SQ, dtype=np.float32)[:, None] * freqs[None, :]
    row = [f for _ in range(2) for f in range(HD) for _ in range(GROUP)]
    cos = np.stack([np.cos(ang[:, f % half]) for f in row]).astype(np.float32)
    sin = np.stack([np.sin(ang[:, f % half]) * (-1 if f < half else 1) for f in row]).astype(np.float32)
    r, c = np.arange(P)[:, None], np.arange(P + WINDOW)[None, :]
    bf16 = mybir.dt.np(BF16)
    near = np.where((r <= c) & (c <= r + WINDOW), 0.0, OUTSIDE)
    first = np.where(c < WINDOW, OUTSIDE, near)
    outside = np.stack([np.concatenate(x, 1) for x in ((first, near), (near, near))], 1).astype(bf16)
    before = (r < np.arange(P)[None, :]).astype(bf16)
    return {
        "cos": cos, "sin": sin, "ident": np.eye(P, dtype=np.float32),
        "ident16": np.eye(P, dtype=bf16), "outside": outside, "before": before,
        "ones16": np.ones((P, P), bf16), "ones_rows": np.ones((4, GROUP * SK), bf16),
        "expert_no": np.tile(np.arange(EXPERTS, dtype=np.float32), TILES),
    }


def lay_out(i):
    t = lambda a: np.ascontiguousarray(np.asarray(a).T)
    a = {k: np.asarray(v) for k, v in i.items()}
    out = {
        "x": a["x"], "ctxT": np.ascontiguousarray(a["ctx_1024"].transpose(0, 2, 1)), "mask": a["mask_BxS2_if1"],
        "wk1": t(a["L1_xattn_W_k"][ORDER]), "wv1": t(a["L1_xattn_W_v"]), "wq1": t(a["L1_xattn_W_q"][ORDER]),
        "wo1": t(a["L1_xattn_W_o"]),
        "wk0": t(a["L0_xattn_k_w"][ORDER]), "wk0p": t(a["L0_xattn_k_w"][PARTNER]),
        "wq0": t(a["L0_xattn_q_w"][ORDER]), "wq0p": t(a["L0_xattn_q_w"][PARTNER]),
        "wv0": t(a["L0_xattn_v_w"]), "wo0": t(a["L0_xattn_o_w"]),
        "bk1": a["L1_xattn_b_k"][ORDER], "bq1": a["L1_xattn_b_q"][ORDER], "bv1": a["L1_xattn_b_v"], "bo1": a["L1_xattn_b_o"],
        "bk0": a["L0_xattn_k_b"][ORDER], "bk0p": a["L0_xattn_k_b"][PARTNER],
        "bq0": a["L0_xattn_q_b"][ORDER], "bq0p": a["L0_xattn_q_b"][PARTNER],
        "bv0": a["L0_xattn_v_b"], "bo0": a["L0_xattn_o_b"],
        "wg": t(a["L1_ffn_Wg"]), "w1": a["L1_ffn_W1"], "b1": a["L1_ffn_b1"], "w2": a["L1_ffn_W2"], "b2": a["L1_ffn_b2"],
        "c0": a["L0_ffn_in_c"],
    }
    for k in ("f", "i", "c"):
        out["rb" + k] = a["L0_ffn_b" + k]
    for k in ("bk1", "bq1", "bk0", "bk0p", "bq0", "bq0p", "rbf", "rbi", "rbc", "c0"):
        out[k] = t(out[k].reshape(KC, P))
    out["b1"] = np.ascontiguousarray(out["b1"].reshape(EXPERTS, HID // P, P).transpose(0, 2, 1))
    out["rbo"] = a["L0_ffn_bo"]
    for k in ("f", "i", "c", "o"):
        out["rw" + k] = t(a["L0_ffn_w" + k])
        out["ru" + k] = t(a["L0_ffn_u" + k])
    return {**out, **shape_constants()}


SCRATCH = {
    "k1": ([STEPS, PART * HD, GROUP * SK], BF16), "q1": ([STEPS, PART * HD, GROUP * SQ], BF16),
    "k0": ([STEPS, PART * HD, GROUP * SQ], BF16), "q0": ([STEPS, PART * HD, GROUP * SQ], BF16),
    "bias1": ([STEPS, 1, SK], BF16), "v1": ([STEPS, SK, GROUP * HD], F32), "v0": ([STEPS, SQ, GROUP * HD], F32),
    "inverse": ([BATCH, HEADS, SQ], F32), "attn0": ([STEPS, P, SQ], F32), "attn1": ([STEPS, P, SQ], F32),
    "x1": ([BATCH, SQ, D], F32), "x2": ([BATCH, SQ, D], F32), "x3": ([BATCH, SQ, D], F32), "xn3": ([BATCH, SQ, D], F32),
    "z": ([BATCH, SQ, D], F32), "xn1T": ([BATCH, D, SQ], F32),
    "cu": ([P, QT * D], F32), "logits": ([BATCH, P, QT * EXPERTS], F32),
    "rows": ([P, TILES * TOPK], U32), "weights": ([P, TILES * TOPK], F32),
    "xbuf": ([EXPERTS * SLOTS, D], F32), "ybuf": ([EXPERTS * SLOTS, D], F32),
}
STAGES = [project_context, window_attention, close_window, recurrence, open_full, full_attention, close_full,
          route, experts, combine]


def run_stages(nc, d, stages):
    for stage in stages:
        Space.semaphores = []
        stage(nc, d)
        nc.clear_and_free_semaphores(Space.semaphores)
        nc.all_engine_barrier()


def build(nc, d):
    for name, (shape, dt) in SCRATCH.items():
        d[name] = nc.dram_tensor(f"scratch_{name}", shape, dt, kind="Internal").ap()
    run_stages(nc, d, STAGES)


def kernel(**inputs):
    import concourse.bacc as bacc
    from concourse.bass_utils import run_bass_kernel_spmd

    nc = bacc.Bacc("TRN2", target_bir_lowering=False, num_devices=1)
    arrays, d = {}, {}
    for name, a in lay_out(inputs).items():
        arrays[f"in_{name}"] = np.ascontiguousarray(a)
        d[name] = nc.dram_tensor(f"in_{name}", a.shape, mybir.dt.from_np(a.dtype), kind="ExternalInput").ap()
    d["out"] = nc.dram_tensor("out", [BATCH, SQ, D], F32, kind="ExternalOutput").ap()
    build(nc, d)
    r = run_bass_kernel_spmd(nc, [arrays], core_ids=[0])
    return r.results[0]["out"]
```
